# Optimizing a Trainium2 kernel written in Bass

```python
import numpy as np
import jax
import jax.numpy as jnp

def _softmax(x, axis=-1):
    return jax.nn.softmax(x, axis=axis)

def _gelu(x):
    return jax.nn.gelu(x, approximate=True)

def _silu(x):
    return jax.nn.silu(x)

def _sigmoid(x):
    return jax.nn.sigmoid(x)

def _layernorm(x, axis=-1, eps=1e-05):
    m = jnp.mean(x, axis=axis, keepdims=True)
    v = jnp.var(x, axis=axis, keepdims=True)
    return (x - m) / jnp.sqrt(v + eps)

def _scatter_add(tgt, idx, src, axis=0):
    return tgt.at[idx].add(src)

def _segment_sum(src, seg, n):
    return jax.ops.segment_sum(src, seg, n)
kernel_name = 'mk_conv_seq_d4_conv_nchw384_r2_b30434'

def setup_inputs(seed: int=0):
    np.random.seed(seed)
    _w = jnp.asarray

    def _rec_inputs():
        import jax
        import jax.numpy as jnp
        _gk = jax.random.key(seed)
        x = -0.0001372 + 0.9999 * jax.random.normal(jax.random.fold_in(_gk, 1), (2, 192, 112, 112), jnp.float32)
        return x
    x = _rec_inputs()

    def _L0_conv_setup():
        import jax, jax.numpy as jnp
        import numpy as np
        WS = 8
        NH = 8

        def _layernorm(x, g, b, eps=1e-05):
            m = x.mean(-1, keepdims=True)
            v = ((x - m) ** 2).mean(-1, keepdims=True)
            return (x - m) * jax.lax.rsqrt(v + eps) * g + b
        key = jax.random.key(seed)
        ks = jax.random.split(key, 6)
        B, C, H, W = (4, 192, 112, 112)
        s = 0.02
        return {'x': jax.random.normal(ks[0], (B, C, H, W), dtype=jnp.float32), 'qkv_w': jax.random.normal(ks[1], (C, 3 * C), dtype=jnp.float32) * s, 'proj_w': jax.random.normal(ks[2], (C, C), dtype=jnp.float32) * s, 'proj_b': jnp.zeros((C,), jnp.float32), 'ln1_g': jnp.ones((C,), jnp.float32), 'ln1_b': jnp.zeros((C,), jnp.float32), 'ln2_g': jnp.ones((C,), jnp.float32), 'ln2_b': jnp.zeros((C,), jnp.float32), 'fc1_w': jax.random.normal(ks[3], (C, 4 * C), dtype=jnp.float32) * s, 'fc1_b': jnp.zeros((4 * C,), jnp.float32), 'fc2_w': jax.random.normal(ks[4], (4 * C, C), dtype=jnp.float32) * s, 'fc2_b': jnp.zeros((C,), jnp.float32)}
    _L0_conv_all = _L0_conv_setup()
    _L0_conv_in = {k: v for k, v in _L0_conv_all.items() if k in ('qkv_w', 'proj_w', 'proj_b', 'ln1_g', 'ln1_b', 'ln2_g', 'ln2_b', 'fc1_w', 'fc1_b', 'fc2_w', 'fc2_b')}
    del _L0_conv_all

    def _L1_conv_setup():
        import jax, jax.numpy as jnp
        import numpy as np
        B, C, H, W = (16, 192, 48, 48)
        EPS = 1e-05

        def _depthwise3x3(x, k2d, channels):
            k = jnp.tile(k2d[None, None, :, :], (channels, 1, 1, 1))
            return jax.lax.conv_general_dilated(x, k, window_strides=(1, 1), padding='SAME', feature_group_count=channels, dimension_numbers=('NCHW', 'OIHW', 'NCHW'))
        key = jax.random.key(seed)
        k1, k2 = jax.random.split(key)
        x = jax.random.normal(k1, (B, C, H, W), dtype=jnp.float32)
        fusion_w = jax.random.normal(k2, (C, 2 * C), dtype=jnp.float32) * 0.02
        fusion_b = jnp.zeros((C,), dtype=jnp.float32)
        ln_w = jnp.ones((C,), dtype=jnp.float32)
        ln_b = jnp.zeros((C,), dtype=jnp.float32)
        return {'x': x, 'fusion_w': fusion_w, 'fusion_b': fusion_b, 'ln_w': ln_w, 'ln_b': ln_b}
    _L1_conv_all = _L1_conv_setup()
    _L1_conv_in = {k: v for k, v in _L1_conv_all.items() if k in ('fusion_w', 'fusion_b', 'ln_w', 'ln_b')}
    del _L1_conv_all

    def _L2_conv_setup():
        import jax, jax.numpy as jnp
        import numpy as np
        DIM = 192
        HID = 4 * DIM
        EPS = 1e-06
        GRN_EPS = 1e-06

        def _block(x, dw_w, dw_b, ln_w, ln_b, w1, b1, grn_gamma, grn_beta, w2, b2):
            identity = x
            y = jax.lax.conv_general_dilated(x, dw_w, window_strides=(1, 1), padding=((3, 3), (3, 3)), dimension_numbers=('NCHW', 'OIHW', 'NCHW'), feature_group_count=DIM)
            y = y + dw_b[None, :, None, None]
            y = jnp.transpose(y, (0, 2, 3, 1))
            mu = jnp.mean(y, axis=-1, keepdims=True)
            var = jnp.mean(jnp.square(y - mu), axis=-1, keepdims=True)
            y = (y - mu) * jax.lax.rsqrt(var + EPS) * ln_w + ln_b
            y = jnp.einsum('bhwc,cd->bhwd', y, w1) + b1
            y = jax.nn.gelu(y, approximate=False)
            gx = jnp.sqrt(jnp.sum(jnp.square(y), axis=(1, 2), keepdims=True))
            nx = gx / (jnp.mean(gx, axis=-1, keepdims=True) + GRN_EPS)
            y = grn_gamma * (y * nx) + grn_beta + y
            y = jnp.einsum('bhwd,dc->bhwc', y, w2) + b2
            return identity + jnp.transpose(y, (0, 3, 1, 2))
        key = jax.random.key(seed)
        ks = jax.random.split(key, 8)
        x = jax.random.normal(ks[0], (16, DIM, 56, 56), dtype=jnp.float32)
        dw_w = jax.random.normal(ks[1], (DIM, 1, 7, 7), dtype=jnp.float32) * 0.02
        dw_b = jnp.zeros((DIM,), dtype=jnp.float32)
        ln_w = jnp.ones((DIM,), dtype=jnp.float32)
        ln_b = jnp.zeros((DIM,), dtype=jnp.float32)
        w1 = jax.random.normal(ks[2], (DIM, HID), dtype=jnp.float32) * 0.02
        b1 = jnp.zeros((HID,), dtype=jnp.float32)
        grn_gamma = jnp.zeros((HID,), dtype=jnp.float32)
        grn_beta = jnp.zeros((HID,), dtype=jnp.float32)
        w2 = jax.random.normal(ks[3], (HID, DIM), dtype=jnp.float32) * 0.02
        b2 = jnp.zeros((DIM,), dtype=jnp.float32)
        return {'x': x, 'dw_w': dw_w, 'dw_b': dw_b, 'ln_w': ln_w, 'ln_b': ln_b, 'w1': w1, 'b1': b1, 'grn_gamma': grn_gamma, 'grn_beta': grn_beta, 'w2': w2, 'b2': b2}
    _L2_conv_all = _L2_conv_setup()
    _L2_conv_in = {k: v for k, v in _L2_conv_all.items() if k in ('dw_w', 'dw_b', 'ln_w', 'ln_b', 'w1', 'b1', 'grn_gamma', 'grn_beta', 'w2', 'b2')}
    del _L2_conv_all

    def _L3_conv_setup():
        import jax, jax.numpy as jnp
        import numpy as np
        from jax import lax
        BN_EPS = 1e-05

        def dwconv(x, w, dilation):
            k = w.shape[-1]
            pad = (dilation * (k - 1) + 1) // 2
            return lax.conv_general_dilated(x, w, window_strides=(1, 1), padding=[(pad, pad), (pad, pad)], rhs_dilation=(dilation, dilation), feature_group_count=x.shape[1], dimension_numbers=('NCHW', 'OIHW', 'NCHW'))

        def bn_eval(y, gamma, beta, mean, var):
            inv = gamma * lax.rsqrt(var + BN_EPS)
            return y * inv[None, :, None, None] + (beta - mean * inv)[None, :, None, None]
        key = jax.random.key(seed)
        ks = jax.random.split(key, 13)
        C = 192
        x = jax.random.normal(ks[0], (16, C, 56, 56), jnp.float32)
        w_lk = jax.random.normal(ks[1], (C, 1, 13, 13), jnp.float32) * 0.05
        w_b0 = jax.random.normal(ks[2], (C, 1, 5, 5), jnp.float32) * 0.05
        w_b1 = jax.random.normal(ks[3], (C, 1, 7, 7), jnp.float32) * 0.05
        w_b2 = jax.random.normal(ks[4], (C, 1, 7, 7), jnp.float32) * 0.05
        w_b3 = jax.random.normal(ks[5], (C, 1, 3, 3), jnp.float32) * 0.05
        w_b4 = jax.random.normal(ks[6], (C, 1, 3, 3), jnp.float32) * 0.05
        w_b5 = jax.random.normal(ks[7], (C, 1, 3, 3), jnp.float32) * 0.05
        bn_gamma = jax.random.uniform(ks[8], (7, C), jnp.float32, 0.5, 1.5)
        bn_beta = jax.random.normal(ks[9], (7, C), jnp.float32) * 0.1
        bn_mean = jax.random.normal(ks[10], (7, C), jnp.float32) * 0.1
        bn_var = jax.random.uniform(ks[11], (7, C), jnp.float32, 0.5, 1.5)
        return dict(x=x, w_lk=w_lk, w_b0=w_b0, w_b1=w_b1, w_b2=w_b2, w_b3=w_b3, w_b4=w_b4, w_b5=w_b5, bn_gamma=bn_gamma, bn_beta=bn_beta, bn_mean=bn_mean, bn_var=bn_var)
    _L3_conv_all = _L3_conv_setup()
    _L3_conv_in = {k: v for k, v in _L3_conv_all.items() if k in ('w_lk', 'w_b0', 'w_b1', 'w_b2', 'w_b3', 'w_b4', 'w_b5', 'bn_gamma', 'bn_beta', 'bn_mean', 'bn_var')}
    del _L3_conv_all
    return {'x': x, 'L0_conv_qkv_w': _L0_conv_in['qkv_w'], 'L0_conv_proj_w': _L0_conv_in['proj_w'], 'L0_conv_proj_b': _L0_conv_in['proj_b'], 'L0_conv_ln1_g': _L0_conv_in['ln1_g'], 'L0_conv_ln1_b': _L0_conv_in['ln1_b'], 'L0_conv_ln2_g': _L0_conv_in['ln2_g'], 'L0_conv_ln2_b': _L0_conv_in['ln2_b'], 'L0_conv_fc1_w': _L0_conv_in['fc1_w'], 'L0_conv_fc1_b': _L0_conv_in['fc1_b'], 'L0_conv_fc2_w': _L0_conv_in['fc2_w'], 'L0_conv_fc2_b': _L0_conv_in['fc2_b'], 'L1_conv_fusion_w': _L1_conv_in['fusion_w'], 'L1_conv_fusion_b': _L1_conv_in['fusion_b'], 'L1_conv_ln_w': _L1_conv_in['ln_w'], 'L1_conv_ln_b': _L1_conv_in['ln_b'], 'L2_conv_dw_w': _L2_conv_in['dw_w'], 'L2_conv_dw_b': _L2_conv_in['dw_b'], 'L2_conv_ln_w': _L2_conv_in['ln_w'], 'L2_conv_ln_b': _L2_conv_in['ln_b'], 'L2_conv_w1': _L2_conv_in['w1'], 'L2_conv_b1': _L2_conv_in['b1'], 'L2_conv_grn_gamma': _L2_conv_in['grn_gamma'], 'L2_conv_grn_beta': _L2_conv_in['grn_beta'], 'L2_conv_w2': _L2_conv_in['w2'], 'L2_conv_b2': _L2_conv_in['b2'], 'L3_conv_w_lk': _L3_conv_in['w_lk'], 'L3_conv_w_b0': _L3_conv_in['w_b0'], 'L3_conv_w_b1': _L3_conv_in['w_b1'], 'L3_conv_w_b2': _L3_conv_in['w_b2'], 'L3_conv_w_b3': _L3_conv_in['w_b3'], 'L3_conv_w_b4': _L3_conv_in['w_b4'], 'L3_conv_w_b5': _L3_conv_in['w_b5'], 'L3_conv_bn_gamma': _L3_conv_in['bn_gamma'], 'L3_conv_bn_beta': _L3_conv_in['bn_beta'], 'L3_conv_bn_mean': _L3_conv_in['bn_mean'], 'L3_conv_bn_var': _L3_conv_in['bn_var']}

def reference(x, L0_conv_qkv_w, L0_conv_proj_w, L0_conv_proj_b, L0_conv_ln1_g, L0_conv_ln1_b, L0_conv_ln2_g, L0_conv_ln2_b, L0_conv_fc1_w, L0_conv_fc1_b, L0_conv_fc2_w, L0_conv_fc2_b, L1_conv_fusion_w, L1_conv_fusion_b, L1_conv_ln_w, L1_conv_ln_b, L2_conv_dw_w, L2_conv_dw_b, L2_conv_ln_w, L2_conv_ln_b, L2_conv_w1, L2_conv_b1, L2_conv_grn_gamma, L2_conv_grn_beta, L2_conv_w2, L2_conv_b2, L3_conv_w_lk, L3_conv_w_b0, L3_conv_w_b1, L3_conv_w_b2, L3_conv_w_b3, L3_conv_w_b4, L3_conv_w_b5, L3_conv_bn_gamma, L3_conv_bn_beta, L3_conv_bn_mean, L3_conv_bn_var):
    import jax
    import jax.numpy as jnp

    def _L0_conv_ref(x, qkv_w, proj_w, proj_b, ln1_g, ln1_b, ln2_g, ln2_b, fc1_w, fc1_b, fc2_w, fc2_b):
        import jax, jax.numpy as jnp
        import numpy as np
        WS = 8
        NH = 8

        def _layernorm(x, g, b, eps=1e-05):
            m = x.mean(-1, keepdims=True)
            v = ((x - m) ** 2).mean(-1, keepdims=True)
            return (x - m) * jax.lax.rsqrt(v + eps) * g + b
        B, C, H, W = x.shape
        ws, nh = (WS, NH)
        hd = C // nh
        scale = hd ** (-0.5)
        N = ws * ws
        xh = jnp.transpose(x, (0, 2, 3, 1))
        xw = xh.reshape(B, H // ws, ws, W // ws, ws, C)
        xw = xw.transpose(0, 1, 3, 2, 4, 5).reshape(-1, N, C)
        h = _layernorm(xw, ln1_g, ln1_b)
        qkv = (h @ qkv_w).reshape(-1, N, 3, nh, hd)
        q, k, v = (qkv[:, :, 0], qkv[:, :, 1], qkv[:, :, 2])
        attn = jax.nn.softmax(jnp.einsum('bnhd,bmhd->bhnm', q, k) * scale, axis=-1)
        o = jnp.einsum('bhnm,bmhd->bnhd', attn, v).reshape(-1, N, C)
        a = o @ proj_w + proj_b + xw
        m = _layernorm(a, ln2_g, ln2_b)
        m = jax.nn.gelu(m @ fc1_w + fc1_b, approximate=False) @ fc2_w + fc2_b + a
        out = m.reshape(B, H // ws, W // ws, ws, ws, C)
        out = out.transpose(0, 1, 3, 2, 4, 5).reshape(B, H, W, C)
        return jnp.transpose(out, (0, 3, 1, 2))

    def _L1_conv_ref(x, fusion_w, fusion_b, ln_w, ln_b):
        import jax, jax.numpy as jnp
        import numpy as np
        B, C, H, W = (16, 192, 48, 48)
        EPS = 1e-05

        def _depthwise3x3(x, k2d, channels):
            k = jnp.tile(k2d[None, None, :, :], (channels, 1, 1, 1))
            return jax.lax.conv_general_dilated(x, k, window_strides=(1, 1), padding='SAME', feature_group_count=channels, dimension_numbers=('NCHW', 'OIHW', 'NCHW'))
        c = x.shape[1]
        sobel_x = jnp.array([[-1.0, 0.0, 1.0], [-2.0, 0.0, 2.0], [-1.0, 0.0, 1.0]], dtype=x.dtype)
        sobel_y = jnp.array([[-1.0, -2.0, -1.0], [0.0, 0.0, 0.0], [1.0, 2.0, 1.0]], dtype=x.dtype)
        edge_x = _depthwise3x3(x, sobel_x, c)
        edge_y = _depthwise3x3(x, sobel_y, c)
        edges = jnp.concatenate([edge_x, edge_y], axis=1)
        fused = jnp.einsum('bchw,oc->bohw', edges, fusion_w) + fusion_b[None, :, None, None]
        mu = jnp.mean(fused, axis=1, keepdims=True)
        var = jnp.mean(jnp.square(fused - mu), axis=1, keepdims=True)
        normed = (fused - mu) * jax.lax.rsqrt(var + EPS)
        normed = normed * ln_w[None, :, None, None] + ln_b[None, :, None, None]
        return x + jax.nn.gelu(normed, approximate=False)

    def _L2_conv_ref(x, dw_w, dw_b, ln_w, ln_b, w1, b1, grn_gamma, grn_beta, w2, b2):
        import jax, jax.numpy as jnp
        import numpy as np
        DIM = 192
        HID = 4 * DIM
        EPS = 1e-06
        GRN_EPS = 1e-06

        def _block(x, dw_w, dw_b, ln_w, ln_b, w1, b1, grn_gamma, grn_beta, w2, b2):
            identity = x
            y = jax.lax.conv_general_dilated(x, dw_w, window_strides=(1, 1), padding=((3, 3), (3, 3)), dimension_numbers=('NCHW', 'OIHW', 'NCHW'), feature_group_count=DIM)
            y = y + dw_b[None, :, None, None]
            y = jnp.transpose(y, (0, 2, 3, 1))
            mu = jnp.mean(y, axis=-1, keepdims=True)
            var = jnp.mean(jnp.square(y - mu), axis=-1, keepdims=True)
            y = (y - mu) * jax.lax.rsqrt(var + EPS) * ln_w + ln_b
            y = jnp.einsum('bhwc,cd->bhwd', y, w1) + b1
            y = jax.nn.gelu(y, approximate=False)
            gx = jnp.sqrt(jnp.sum(jnp.square(y), axis=(1, 2), keepdims=True))
            nx = gx / (jnp.mean(gx, axis=-1, keepdims=True) + GRN_EPS)
            y = grn_gamma * (y * nx) + grn_beta + y
            y = jnp.einsum('bhwd,dc->bhwc', y, w2) + b2
            return identity + jnp.transpose(y, (0, 3, 1, 2))
        return _block(x, dw_w, dw_b, ln_w, ln_b, w1, b1, grn_gamma, grn_beta, w2, b2)

    def _L3_conv_ref(x, w_lk, w_b0, w_b1, w_b2, w_b3, w_b4, w_b5, bn_gamma, bn_beta, bn_mean, bn_var):
        import jax, jax.numpy as jnp
        import numpy as np
        from jax import lax
        BN_EPS = 1e-05

        def dwconv(x, w, dilation):
            k = w.shape[-1]
            pad = (dilation * (k - 1) + 1) // 2
            return lax.conv_general_dilated(x, w, window_strides=(1, 1), padding=[(pad, pad), (pad, pad)], rhs_dilation=(dilation, dilation), feature_group_count=x.shape[1], dimension_numbers=('NCHW', 'OIHW', 'NCHW'))

        def bn_eval(y, gamma, beta, mean, var):
            inv = gamma * lax.rsqrt(var + BN_EPS)
            return y * inv[None, :, None, None] + (beta - mean * inv)[None, :, None, None]
        dilates = (1, 1, 2, 3, 4, 5)
        branch_ws = (w_b0, w_b1, w_b2, w_b3, w_b4, w_b5)
        out = bn_eval(dwconv(x, w_lk, 1), bn_gamma[0], bn_beta[0], bn_mean[0], bn_var[0])
        for i, (w, r) in enumerate(zip(branch_ws, dilates)):
            j = i + 1
            out = out + bn_eval(dwconv(x, w, r), bn_gamma[j], bn_beta[j], bn_mean[j], bn_var[j])
        return out

    def _gn(v, G=32, eps=1e-05):
        B_, C_, H_, W_ = v.shape
        g = v.reshape(B_, G, C_ // G, H_, W_)
        m = jnp.mean(g, axis=(2, 3, 4), keepdims=True)
        s = jnp.var(g, axis=(2, 3, 4), keepdims=True)
        return ((g - m) / jnp.sqrt(s + eps)).reshape(v.shape)

    def _ln_c(v, eps=1e-06):
        m = jnp.mean(v, axis=1, keepdims=True)
        s = jnp.var(v, axis=1, keepdims=True)
        return (v - m) / jnp.sqrt(s + eps)

    def _ln_t(v, eps=1e-05):
        m = jnp.mean(v, axis=-1, keepdims=True)
        s = jnp.var(v, axis=-1, keepdims=True)
        return (v - m) / jnp.sqrt(s + eps)

    def _to_tokens(v):
        B_, C_, H_, W_ = v.shape
        return v.reshape(B_, C_, H_ * W_).transpose(0, 2, 1)

    def _from_tokens(t, like):
        B_, C_, H_, W_ = like.shape
        return t.transpose(0, 2, 1).reshape(B_, C_, H_, W_)
    x = _L0_conv_ref(x, L0_conv_qkv_w, L0_conv_proj_w, L0_conv_proj_b, L0_conv_ln1_g, L0_conv_ln1_b, L0_conv_ln2_g, L0_conv_ln2_b, L0_conv_fc1_w, L0_conv_fc1_b, L0_conv_fc2_w, L0_conv_fc2_b)
    x = _L1_conv_ref(x, L1_conv_fusion_w, L1_conv_fusion_b, L1_conv_ln_w, L1_conv_ln_b)
    x = _L2_conv_ref(x, L2_conv_dw_w, L2_conv_dw_b, L2_conv_ln_w, L2_conv_ln_b, L2_conv_w1, L2_conv_b1, L2_conv_grn_gamma, L2_conv_grn_beta, L2_conv_w2, L2_conv_b2)
    x = _L3_conv_ref(x, L3_conv_w_lk, L3_conv_w_b0, L3_conv_w_b1, L3_conv_w_b2, L3_conv_w_b3, L3_conv_w_b4, L3_conv_w_b5, L3_conv_bn_gamma, L3_conv_bn_beta, L3_conv_bn_mean, L3_conv_bn_var)
    return x

_drawn_inputs = setup_inputs


def setup_inputs(seed=0):
    import zlib

    import numpy as np

    out = dict(_drawn_inputs(seed))
    spreads = {'L0_conv_proj_b': (0.0, 0.1),
     'L0_conv_ln1_g': (1.0, 0.6),
     'L0_conv_ln1_b': (0.0, 0.8),
     'L0_conv_ln2_g': (1.0, 0.6),
     'L0_conv_ln2_b': (0.0, 2.0),
     'L0_conv_fc1_b': (0.0, 0.328),
     'L0_conv_fc2_b': (0.0, 0.1),
     'L1_conv_fusion_b': (0.0, 0.8),
     'L1_conv_ln_w': (1.0, 0.2),
     'L1_conv_ln_b': (0.0, 0.383),
     'L2_conv_dw_b': (0.0, 0.455),
     'L2_conv_ln_w': (1.0, 0.6),
     'L2_conv_ln_b': (0.0, 0.8),
     'L2_conv_b1': (0.0, 0.349),
     'L2_conv_grn_gamma': (0.0, 0.8),
     'L2_conv_grn_beta': (0.0, 0.485),
     'L2_conv_b2': (0.0, 0.1)}
    factors = {'L0_conv_qkv_w': 5.118, 'L0_conv_proj_w': 5.392}
    for name, (base, spread) in spreads.items():
        noise = np.random.default_rng([zlib.crc32(name.encode()), seed]).standard_normal(out[name].shape)
        drawn = base * np.exp(spread * noise) if base else spread * noise
        out[name] = jnp.asarray(drawn.astype(out[name].dtype))
    for name, factor in factors.items():
        out[name] = (out[name] * factor).astype(out[name].dtype)
    return out
```

```python
import concourse.bass as bass
from concourse import mybir
from contextlib import ExitStack

F32 = mybir.dt.float32
ALU = mybir.AluOpType
ACT = mybir.ActivationFunctionType
AX = mybir.AxisListType

C = 192
KC = 2
CH = C // KC
HID = 4 * C
MC = HID // 128
IMG, BY, BX = 2, 14, 7
HW = 112
PER = BY * BX
NB = IMG * PER
NS = IMG * BY
NH, HD = 8, 24
ROW = HW * 8

KW = 13
GP = 40
GROWS = 32
GSZ = GROWS * GP
GRUN = 24 * GP
GR0 = 9
GC0 = (9, 1)
GWRAP = 33
WRAPC = 6


class Step:

    def __init__(self, g, j, unroll):
        self.g, self.j, self.unroll = g, j, unroll

    def back(self, lag):
        return Step(self.g, self.j - lag, self.unroll)

    @property
    def n(self):
        return self.g * self.unroll + self.j

    def upto(self, k):
        return min(self.n + k, NB) if self.fixed else self.n + k

    @property
    def fixed(self):
        return isinstance(self.g, int)

    def reached(self, k):
        return not self.fixed or self.n >= k

    def inside(self, count):
        return not self.fixed or 0 <= self.n < count

    def buf(self, ring):
        return self.j % ring

    def turn(self, ring):
        return self.g * (self.unroll // ring) + self.j // ring


def run_steps(eng, count, unroll, head, lag, body):
    assert (count - head) % unroll == 0
    for j in range(head):
        body(Step(0, j, unroll))
    with eng.Fori(0, (count - head) // unroll) as g:
        for j in range(unroll):
            body(Step(g, head + j, unroll))
    for j in range(count, count + lag):
        body(Step(0, j, unroll))


def at_hand(eng, value):
    return value if isinstance(value, int) else eng.snap(eng.to_reg(value))


def view(ap, dims, shift=0):
    return bass.AP(ap.tensor, ap.offset + shift, [list(ap.ap[0])] + [list(d) for d in dims])


def at(ap, i):
    return ap[:, bass.ds(i, 1)].rearrange("p o c -> p (o c)")


class Scope:

    def __init__(self, nc, tag, stack):
        self.nc, self.tag, self.stack = nc, tag, stack

    def sb(self, name, shape):
        return self.stack.enter_context(self.nc.sbuf_tensor(f"{self.tag}_{name}", shape, F32))

    def sem(self, name):
        return self.nc.alloc_semaphore(f"{self.tag}_{name}")

    def sems(self, name, n):
        return [self.sem(f"{name}{i}") for i in range(n)]


def prepare(nc, a, d, stack):
    s = Scope(nc, "prep", stack)
    taps = ["w_lk", "w_b0", "w_b1", "w_b2", "w_b3", "w_b4", "w_b5"]
    dilation = [1, 1, 1, 2, 3, 4, 5]
    side = [13, 5, 7, 7, 3, 3, 3]
    wt = [s.sb(f"taps{i}", [CH, KC, k, k]) for i, k in enumerate(side)]
    w7 = s.sb("taps7", [CH, KC, 7, 7])
    bn = s.sb("bn", [CH, 4, KC, 7])
    merged = s.sb("merged", [CH, KC, KW, KW])
    inv = s.sb("inv", [CH, KC, 7])
    half = s.sb("half", [CH, KC, 7])
    shift = s.sb("shift", [CH, KC, 7])
    bias = s.sb("bias", [CH, KC])
    zrow = s.sb("zrow", [CH, KC, HW])
    padded = [[s.sb(f"pad{i}{h}", [CH, KC, GSZ]) for h in range(2)] for i in range(2)]
    loaded, var_ok, inv_ok, zeroed, built, biased, stored, chain, cleared = (
        s.sem(x) for x in ("loaded", "var_ok", "inv_ok", "zeroed", "built", "biased", "stored", "chain", "cleared"))
    nload = len(taps) + 1 + 4

    with nc.Block() as block:
        @block.sync
        def _(sp):
            for t, name in zip(wt, taps):
                sp.dma_start(t[:, :, :, :], a["L3_conv_" + name].rearrange("(k p) o y x -> p k (o y) x", k=KC)).then_inc(loaded, 16)
            sp.dma_start(w7[:, :, :, :], a["L2_conv_dw_w"].rearrange("(k p) o y x -> p k (o y) x", k=KC)).then_inc(loaded, 16)
            for i, name in enumerate(("gamma", "beta", "mean", "var")):
                sp.dma_start(bn[:, i, :, :], a["L3_conv_bn_" + name].rearrange("(k p) j -> p k j", k=KC)).then_inc(loaded, 16)
            sp.wait_ge(zeroed, 1)
            for img in range(IMG):
                for r in (0, HW + 1):
                    sp.dma_start(d["x1"][img, :, r, :].rearrange("(k p) x -> p k x", k=KC), zrow[:, :, :]).then_inc(stored, 16)
            sp.wait_ge(built, 1)
            for i in range(2):
                for h in range(2):
                    sp.dma_start(d["taps"][i, h].rearrange("(k p) g -> p k g", k=KC), padded[i][h][:, :, :]).then_inc(stored, 16)
            sp.wait_ge(biased, 1)
            sp.dma_start(d["bias"].rearrange("(k p) -> p k", k=KC), bias[:, :]).then_inc(stored, 16)
            sp.wait_ge(stored, 16 * (2 * IMG + 4 + 1))

        @block.gpsimd
        def _(pool):
            nc.gpsimd.memset(zrow[:, :, :], 0.0).then_inc(zeroed, 1)
            nc.gpsimd.memset(half[:, :, :], -0.5).then_inc(cleared, 1)
            for i in range(2):
                for h in range(2):
                    nc.gpsimd.memset(padded[i][h][:, :, :], 0.0).then_inc(cleared, 1)
            pool.wait_ge(loaded, 16 * nload)
            nc.gpsimd.tensor_scalar(bn[:, 3], bn[:, 3], 1e-5, None, ALU.add).then_inc(var_ok, 1)
            pool.wait_ge(var_ok, 1)
            pool.wait_ge(cleared, 1)
            nc.gpsimd.tensor_tensor(inv[:, :, :], bn[:, 3], half[:, :, :], ALU.pow).then_inc(inv_ok, 1)

        @block.vector
        def _(dve):
            done = [0]

            def then(ins):
                done[0] += 1
                ins.then_inc(chain, 1)
                dve.wait_ge(chain, done[0])

            dve.wait_ge(loaded, 16 * nload)
            dve.wait_ge(inv_ok, 1)
            dve.wait_ge(cleared, 5)
            then(nc.vector.tensor_tensor(inv[:, :, :], inv[:, :, :], bn[:, 0], ALU.mult))
            then(nc.vector.tensor_tensor(shift[:, :, :], inv[:, :, :], bn[:, 2], ALU.mult))
            then(nc.vector.tensor_tensor(shift[:, :, :], bn[:, 1], shift[:, :, :], ALU.subtract))
            nc.vector.reduce_sum(bias[:, :], shift[:, :, :], AX.X).then_inc(biased, 1)
            for k in range(KC):
                then(nc.vector.tensor_scalar(merged[:, k], wt[0][:, k], inv[:, k, 0:1], None, ALU.mult))
                for j in range(1, 7):
                    lo, st = KW // 2 - side[j] // 2 * dilation[j], dilation[j]
                    sub = merged[:, k, lo:KW - lo:st, lo:KW - lo:st]
                    then(nc.vector.scalar_tensor_tensor(sub, wt[j][:, k], inv[:, k, j:j + 1], sub, ALU.mult, ALU.add))
            for i, (src, side_i) in enumerate(((w7, 7), (merged, KW))):
                off = (KW - side_i) // 2
                for h in range(2):
                    for k in range(KC):
                        rows = padded[i][h][:, k, :].rearrange("p (r g) -> p r g", g=GP)[:, GR0 + off:GR0 + off + side_i]
                        then(nc.vector.tensor_copy(rows[:, :, GC0[h] + off:GC0[h] + off + side_i], src[:, k]))
                        if h:
                            n = WRAPC - off
                            then(nc.vector.tensor_copy(rows[:, :, GWRAP + off:GWRAP + off + n], src[:, k, :, 0:n]))
            nc.vector.nop().then_inc(built, 1)


def attention(nc, a, d, X, PS, stack):
    s = Scope(nc, "att", stack)
    XR, XB = 4, 12
    wqk = s.sb("wqk", [CH, KC, 4, 4, 32])
    wv = s.sb("wv", [CH, KC, C])
    wp = s.sb("wp", [CH, KC, C])
    gb = s.sb("gb", [CH, 2, KC])
    pb = s.sb("pb", [128, C])
    ident = s.sb("ident", [128, 128])
    x = s.sb("x", [128, XR, C])
    st = s.sb("st", [128, 2, 6])
    mv = s.sb("mv", [128, 4, 2])
    ve = s.sb("ve", [128, 2])
    rs = s.sb("rs", [128, 4])
    mhalf = s.sb("mhalf", [128, 1])
    xn = s.sb("xn", [128, 2, C])
    xpb = s.sb("xpb", [128, XB, C])
    h = s.sb("h", [CH, 2, KC, 128])
    qk = s.sb("qk", [128, 2, 4, 128])
    vbd = s.sb("vbd", [128, 6, 2, 4, 2, HD + 1])
    mx = s.sb("mx", [128, 2, NH])
    sd = s.sb("sd", [128, 2, 512])
    p = s.sb("p", [128, 4, 512])
    pt = s.sb("pt", [128, 2, 4, 128])
    ri = s.sb("ri", [128, 2, NH])
    o = s.sb("o", [128, 2, C])
    ot = s.sb("ot", [CH, 2, KC, 128])

    psS = PS[:, 0:4, 0:128]
    psPV = PS[:, 0, 128:328]
    psPJ = PS[:, 1, 128:128 + C]
    psT = PS[0:CH, 7, 0:256]
    psOT = PS[0:CH, 7, 256:512]
    psQK = PS[:, 5, :]
    psV = PS[:, 6, 0:C]
    psPT = PS[:, 4, :]

    wloaded, ready, loaded = s.sem("wloaded"), s.sem("ready"), s.sems("loaded", XR)
    names = ("stats", "aggr", "var_ok", "rstd", "xn_ready", "xt", "h_ready", "qk", "qk_ready", "v", "v_ready",
             "scores", "max", "shifted", "probs", "pt", "pt_ready", "pv", "recip", "o_ready", "ot", "ot_ready",
             "proj", "resid", "xpb_ready")
    q = {x: s.sem(x) for x in names}
    READY = 5 + 6 * 2
    HEAD, LAG, U = 16, 9, 12

    with nc.Block() as block:
        @block.sync
        def _(sp):
            nc.sync.dma_start(wv[:, :, :], a["L0_conv_qkv_w"].rearrange("(k p) n -> p k n", k=KC)[:, :, 2 * C:3 * C]).then_inc(wloaded, 16)
            nc.sync.dma_start(wp[:, :, :], a["L0_conv_proj_w"].rearrange("(k p) n -> p k n", k=KC)).then_inc(wloaded, 16)
            nc.sync.dma_start(gb[:, 0, :], a["L0_conv_ln1_g"].rearrange("(k p) -> p k", k=KC)).then_inc(wloaded, 16)
            nc.sync.dma_start(gb[:, 1, :], a["L0_conv_ln1_b"].rearrange("(k p) -> p k", k=KC)).then_inc(wloaded, 16)
            nc.sync.dma_start(pb[:, :], a["L0_conv_proj_b"].partition_broadcast(128)).then_inc(wloaded, 16)
            sp.wait_ge(ready, 1)
            for k in range(KC):
                for ch in range(4):
                    src = a["L0_conv_qkv_w"][k * CH:(k + 1) * CH, ch * CH:(ch + 1) * CH].rearrange("p (h e) -> p h e", e=HD)
                    nc.sync.dma_start(wqk[:, k, ch, :, 0:HD], src).then_inc(wloaded, 16)

            def body(t):
                if t.reached(XR):
                    sp.wait_ge(q["xn_ready"], t.n - XR + 1)
                    sp.wait_ge(q["xpb_ready"], t.n - XR + 1)
                sp.dma_start(x[:, t.buf(XR), :], d["x"][bass.ds(t.n, 1)].rearrange("o p c -> (o p) c")).then_inc(loaded[t.buf(XR)], 16)
            run_steps(sp, NB, U, HEAD, 0, body)

        @block.gpsimd
        def _(pool):
            nc.gpsimd.memset(wqk[:, :, :, :, :], 0.0).then_inc(ready, 1)
            nc.gpsimd.memset(mhalf[:, :], -0.5).then_inc(ready, 1)
            nc.gpsimd.memset(ident[:, :], 0.0).then_inc(ready, 1)
            nc.gpsimd.memset(vbd[:, :, :, :, :, :], 0.0).then_inc(ready, 1)
            pool.wait_ge(ready, 4)
            nc.gpsimd.affine_select(out=ident[:, :], in_=ident[:, :], compare_op=ALU.not_equal, fill=1.0, base=0,
                                    pattern=[[-1, 128]], channel_multiplier=1).then_inc(ready, 1)
            pool.wait_ge(wloaded, 16 * 13)

            def body(t):
                if t.inside(NB):
                    reached = at_hand(pool, t.n + 1)
                    pool.wait_ge(ready, READY)
                    pool.wait_ge(q["aggr"], reached)
                    nc.gpsimd.tensor_scalar(ve[:, t.buf(2):t.buf(2) + 1], mv[:, t.buf(4), 1:2], 1e-5, None, ALU.add).then_inc(q["var_ok"], 1)
                    pool.wait_ge(q["var_ok"], t.n + 1)
                    if t.reached(4):
                        pool.wait_ge(q["xn_ready"], t.n - 3)
                    nc.gpsimd.tensor_tensor(rs[:, t.buf(4):t.buf(4) + 1], ve[:, t.buf(2):t.buf(2) + 1], mhalf[:, :], ALU.pow).then_inc(q["rstd"], 1)
                    if t.reached(XB):
                        pool.wait_ge(q["resid"], t.n - XB + 1)
                    nc.gpsimd.tensor_tensor(xpb[:, t.buf(XB), :], x[:, t.buf(XR), :], pb[:, :], ALU.add).then_inc(q["xpb_ready"], 1)
            run_steps(pool, NB, U, HEAD, 0, body)

        @block.vector
        def _(dve):
            dve.wait_ge(ready, 5)
            for b in range(6):
                for e in range(2):
                    nc.vector.memset(vbd[64 * e:64 * e + 64, b, :, :, e, HD:HD + 1], 1.0).then_inc(ready, 1)

            def body(t):
                b = t.back(4)
                if b.inside(NB):
                    dve.wait_ge(q["scores"], b.n + 1)
                    s4 = psS.rearrange("p h (e m) -> p h e m", e=2)
                    nc.vector.reduce_max(mx[:, b.buf(2), :].rearrange("p (h e) -> p h e", e=2), s4, AX.X).then_inc(q["max"], 1)
                    dve.wait_ge(q["max"], b.n + 1)
                    if b.reached(2):
                        dve.wait_ge(q["probs"], b.n - 1)
                    nc.vector.tensor_tensor(sd[:, b.buf(2), :].rearrange("p (h e m) -> p h e m", h=4, e=2), s4,
                                            view(mx[:, b.buf(2), :], [[2, 4], [1, 2], [0, 64]]), ALU.subtract).then_inc(q["shifted"], 1)
                b = t.back(1)
                if b.inside(NB):
                    dve.wait_ge(q["rstd"], b.n + 1)
                    if b.reached(2):
                        dve.wait_ge(q["xt"], b.n - 1)
                    nc.vector.tensor_scalar(xn[:, b.buf(2), :], x[:, b.buf(XR), :], mv[:, b.buf(4), 0:1], rs[:, b.buf(4):b.buf(4) + 1],
                                            ALU.subtract, ALU.mult).then_inc(q["xn_ready"], 1)
                b = t
                if b.inside(NB):
                    dve.wait_ge(loaded[b.buf(XR)], 16 * (b.turn(XR) + 1))
                    nc.vector.bn_stats(out=st[:, b.buf(2), :], in_=x[:, b.buf(XR), :]).then_inc(q["stats"], 1)
                    reached = at_hand(dve, b.n + 1)
                    dve.wait_ge(ready, READY)
                    dve.wait_ge(q["stats"], reached)
                    nc.vector.bn_aggr(out=mv[:, b.buf(4), :], in_=st[:, b.buf(2), :]).then_inc(q["aggr"], 1)
                b = t.back(9)
                if b.inside(NB):
                    dve.wait_ge(q["proj"], b.n + 1)
                    dve.wait_ge(q["xpb_ready"], b.n + 1)
                    nc.vector.tensor_tensor(at(X, b.n), psPJ, xpb[:, b.buf(XB), :], ALU.add).then_inc(q["resid"], 1)
                b = t.back(7)
                if b.inside(NB):
                    dve.wait_ge(q["pv"], b.n + 1)
                    o4 = psPV.rearrange("p (h e c) -> p h e c", h=4, e=2)
                    nc.vector.reciprocal(ri[:, b.buf(2), :].rearrange("p (h e o) -> p h e o", e=2, o=1), o4[:, :, :, HD:HD + 1]).then_inc(q["recip"], 1)
                    dve.wait_ge(q["recip"], b.n + 1)
                    if b.reached(2):
                        dve.wait_ge(q["ot"], b.n - 1)
                    nc.vector.tensor_tensor(o[:, b.buf(2), :].rearrange("p (e h c) -> p h e c", h=4, e=2), o4[:, :, :, 0:HD],
                                            view(ri[:, b.buf(2), :], [[2, 4], [1, 2], [0, HD]]), ALU.mult).then_inc(q["o_ready"], 1)
                b = t.back(6)
                if b.inside(NB):
                    dve.wait_ge(q["pt"], b.n + 1)
                    if b.reached(2):
                        dve.wait_ge(q["pv"], b.n - 1)
                    nc.vector.tensor_copy(pt[:, b.buf(2), :, :].rearrange("p h n -> p (h n)"), psPT).then_inc(q["pt_ready"], 1)
            run_steps(dve, NB, U, HEAD, LAG, body)

        @block.scalar
        def _(act):
            act.wait_ge(wloaded, 16 * 13)
            act.wait_ge(ready, READY)

            def body(t):
                b = t.back(2)
                if b.inside(NB):
                    act.wait_ge(q["xt"], b.n + 1)
                    if b.reached(2):
                        act.wait_ge(q["v"], b.n - 1)
                    for k in range(KC):
                        last = nc.scalar.activation(h[:, b.buf(2), k, :], psT[:, k * 128:(k + 1) * 128],
                                                    ACT.Identity, bias=gb[:, 1, k:k + 1], scale=gb[:, 0, k:k + 1])
                    last.then_inc(q["h_ready"], 1)
                b = t.back(4)
                if b.inside(NB):
                    act.wait_ge(q["shifted"], b.n + 1)
                    if b.reached(4):
                        act.wait_ge(q["pt"], b.n - 3)
                    nc.scalar.activation(p[:, b.buf(4), :], sd[:, b.buf(2), :], ACT.Exp, scale=float(HD) ** -0.5).then_inc(q["probs"], 1)
                b = t.back(3)
                if b.inside(NB):
                    act.wait_ge(q["qk"], b.n + 1)
                    if b.reached(2):
                        act.wait_ge(q["scores"], b.n - 1)
                    nc.scalar.activation(qk[:, b.buf(2), :, :], psQK.rearrange("p (c n) -> p c n", c=4), ACT.Identity).then_inc(q["qk_ready"], 1)
                    act.wait_ge(q["v"], b.n + 1)
                    if b.reached(6):
                        act.wait_ge(q["pv"], b.n - 5)
                    for w in range(2):
                        for e in range(2):
                            src = psV[64 * w:64 * w + 64, :].rearrange("p (e h c) -> p e h c", e=2, h=4)[:, e]
                            last = nc.scalar.activation(vbd[64 * e:64 * e + 64, b.buf(6), w, :, e, 0:HD], src, ACT.Identity)
                    last.then_inc(q["v_ready"], 1)
                b = t.back(8)
                if b.inside(NB):
                    act.wait_ge(q["ot"], b.n + 1)
                    if b.reached(2):
                        act.wait_ge(q["proj"], b.n - 1)
                    nc.scalar.activation(ot[:, b.buf(2), :, :], psOT.rearrange("p (k n) -> p k n", k=KC), ACT.Identity).then_inc(q["ot_ready"], 1)
            run_steps(act, NB, U, HEAD, LAG, body)

        @block.tensor
        def _(pe):
            pe.wait_ge(wloaded, 16 * 13)
            pe.wait_ge(ready, READY)

            def body(t):
                b = t.back(4)
                if b.inside(NB):
                    pe.wait_ge(q["qk_ready"], b.n + 1)
                    if b.reached(1):
                        pe.wait_ge(q["shifted"], b.n)
                    if b.reached(6):
                        pe.wait_ge(q["resid"], b.n - 5)
                    if b.reached(4):
                        pe.wait_ge(q["o_ready"], b.n - 3)
                    for e in range(2):
                        for w in range(2):
                            for hh in range(4):
                                rows = qk[32 * hh:32 * hh + HD, b.buf(2), :, 64 * w:64 * w + 64]
                                last = nc.tensor.matmul(psS[64 * w:64 * w + 64, hh, 64 * e:64 * e + 64], rows[:, e, :], rows[:, 2 + e, :], start=True, stop=True)
                    last.then_inc(q["scores"], 1)
                b = t.back(2)
                if b.inside(NB):
                    pe.wait_ge(q["xn_ready"], b.n + 1)
                    if b.reached(1):
                        pe.wait_ge(q["h_ready"], b.n)
                    if b.reached(7):
                        pe.wait_ge(q["ot_ready"], b.n - 6)
                    for k in range(KC):
                        last = nc.tensor.transpose(psT[:, k * 128:(k + 1) * 128], xn[:, b.buf(2), k * CH:(k + 1) * CH], ident[:, :])
                    last.then_inc(q["xt"], 1)
                b = t.back(3)
                if b.inside(NB):
                    pe.wait_ge(q["h_ready"], b.n + 1)
                    if b.reached(1):
                        pe.wait_ge(q["qk_ready"], b.n)
                    for ch in range(4):
                        for k in range(KC):
                            last = nc.tensor.matmul(psQK[:, ch * 128:(ch + 1) * 128], wqk[:, k, ch, :, :].rearrange("p h e -> p (h e)"),
                                                    h[:, b.buf(2), k, :], start=(k == 0), stop=(k == KC - 1))
                    last.then_inc(q["qk"], 1)
                b = t.back(9)
                if b.inside(NB):
                    pe.wait_ge(q["ot_ready"], b.n + 1)
                    if b.reached(1):
                        pe.wait_ge(q["resid"], b.n)
                    pe.wait_ge(q["shifted"], b.upto(6))
                    for k in range(KC):
                        last = nc.tensor.matmul(psPJ, ot[:, b.buf(2), k, :], wp[:, k, :], start=(k == 0), stop=(k == KC - 1))
                    last.then_inc(q["proj"], 1)
                b = t.back(7)
                if b.inside(NB):
                    pe.wait_ge(q["pt_ready"], b.n + 1)
                    pe.wait_ge(q["v_ready"], b.n + 1)
                    if b.reached(1):
                        pe.wait_ge(q["o_ready"], b.n)
                    pe.wait_ge(q["shifted"], b.upto(4))
                    for w in range(2):
                        for hp in range(4):
                            last = nc.tensor.matmul(psPV[64 * w:64 * w + 64, hp * 50:hp * 50 + 50], pt[:, b.buf(2), hp, 64 * w:64 * w + 64],
                                                    vbd[:, b.buf(6), w, hp, :, :].rearrange("p e c -> p (e c)"), start=True, stop=True)
                    last.then_inc(q["pv"], 1)
                b = t.back(3)
                if b.inside(NB):
                    if b.reached(1):
                        pe.wait_ge(q["v_ready"], b.n)
                    for k in range(KC):
                        last = nc.tensor.matmul(psV, h[:, b.buf(2), k, :], wv[:, k, :], start=(k == 0), stop=(k == KC - 1))
                    last.then_inc(q["v"], 1)
                b = t.back(8)
                if b.inside(NB):
                    pe.wait_ge(q["o_ready"], b.n + 1)
                    if b.reached(1):
                        pe.wait_ge(q["ot_ready"], b.n)
                    pe.wait_ge(q["h_ready"], b.upto(7))
                    for k in range(KC):
                        last = nc.tensor.transpose(psOT[:, k * 128:(k + 1) * 128], o[:, b.buf(2), k * CH:(k + 1) * CH], ident[:, :])
                    last.then_inc(q["ot"], 1)
                b = t.back(6)
                if b.inside(NB):
                    pe.wait_ge(q["probs"], b.n + 1)
                    if b.reached(1):
                        pe.wait_ge(q["pt_ready"], b.n)
                    for hp in range(4):
                        last = nc.tensor.transpose(psPT[:, hp * 128:hp * 128 + 128], p[:, b.buf(4), hp * 128:hp * 128 + 128], ident[:, :])
                    last.then_inc(q["pt"], 1)
            run_steps(pe, NB, U, HEAD, LAG, body)


class NormUp:

    def __init__(self, nc, s, X, PS, eps, hring):
        self.nc, self.X, self.eps, self.hring = nc, X, eps, hring
        self.w1 = s.sb("w1", [CH, KC, HID])
        self.b1 = s.sb("b1", [128, MC])
        self.gb = s.sb("gb", [CH, 2, KC])
        self.ident = s.sb("ident", [128, 128])
        self.st = s.sb("st", [128, 2, 6])
        self.mv = s.sb("mv", [128, 2, 2])
        self.ve = s.sb("ve", [128, 2])
        self.rs = s.sb("rs", [128, 2])
        self.mhalf = s.sb("mhalf", [128, 1])
        self.xn = s.sb("xn", [128, 2, C])
        self.h = s.sb("h", [CH, 2, KC, 128])
        self.hid = s.sb("hid", [128, hring, MC, 128])
        self.psU = [PS[:, 2 * i:2 * i + 2, :].rearrange("p b n -> p (b n)") for i in range(2)]
        self.psT = PS[0:CH, 4, 0:256]
        self.q = {x: s.sem(x) for x in ("ready", "loaded", "stats", "aggr", "var_ok", "rstd", "xn_ready", "xt", "h_ready", "up", "hid_ready")}

    def load(self, eng, w, b, g, shift):
        for dst, src in ((self.w1[:, :, :], w.rearrange("(k p) n -> p k n", k=KC)), (self.b1[:, :], b.rearrange("(m p) -> p m", m=MC)),
                         (self.gb[:, 0, :], g.rearrange("(k p) -> p k", k=KC)), (self.gb[:, 1, :], shift.rearrange("(k p) -> p k", k=KC))):
            eng.dma_start(dst, src).then_inc(self.q["loaded"], 16)

    def constants(self, pool):
        self.nc.gpsimd.memset(self.mhalf[:, :], -0.5).then_inc(self.q["ready"], 1)
        self.nc.gpsimd.memset(self.ident[:, :], 0.0).then_inc(self.q["ready"], 1)
        pool.wait_ge(self.q["ready"], 2)
        self.nc.gpsimd.affine_select(out=self.ident[:, :], in_=self.ident[:, :], compare_op=ALU.not_equal, fill=1.0, base=0,
                                     pattern=[[-1, 128]], channel_multiplier=1).then_inc(self.q["ready"], 1)

    def wait_weights(self, eng):
        eng.wait_ge(self.q["loaded"], 16 * 4)
        eng.wait_ge(self.q["ready"], 3)

    def stats(self, dve, b):
        nc, q = self.nc, self.q
        nc.vector.bn_stats(out=self.st[:, b.buf(2), :], in_=at(self.X, b.n)).then_inc(q["stats"], 1)
        reached = at_hand(dve, b.n + 1)
        dve.wait_ge(q["ready"], 3)
        dve.wait_ge(q["stats"], reached)
        nc.vector.bn_aggr(out=self.mv[:, b.buf(2), :], in_=self.st[:, b.buf(2), :]).then_inc(q["aggr"], 1)

    def rstd(self, pool, b):
        nc, q = self.nc, self.q
        one = slice(b.buf(2), b.buf(2) + 1)
        reached = at_hand(pool, b.n + 1)
        pool.wait_ge(q["ready"], 3)
        pool.wait_ge(q["aggr"], reached)
        nc.gpsimd.tensor_scalar(self.ve[:, one], self.mv[:, b.buf(2), 1:2], self.eps, None, ALU.add).then_inc(q["var_ok"], 1)
        pool.wait_ge(q["var_ok"], b.n + 1)
        if b.reached(2):
            pool.wait_ge(q["xn_ready"], b.n - 1)
        nc.gpsimd.tensor_tensor(self.rs[:, one], self.ve[:, one], self.mhalf[:, :], ALU.pow).then_inc(q["rstd"], 1)

    def normalize(self, dve, b):
        nc, q = self.nc, self.q
        dve.wait_ge(q["rstd"], b.n + 1)
        if b.reached(2):
            dve.wait_ge(q["xt"], b.n - 1)
        nc.vector.tensor_scalar(self.xn[:, b.buf(2), :], at(self.X, b.n), self.mv[:, b.buf(2), 0:1], self.rs[:, b.buf(2):b.buf(2) + 1],
                                ALU.subtract, ALU.mult).then_inc(q["xn_ready"], 1)

    def transpose(self, pe, b):
        nc, q = self.nc, self.q
        pe.wait_ge(q["xn_ready"], b.n + 1)
        if b.reached(1):
            pe.wait_ge(q["h_ready"], b.n)
        for k in range(KC):
            last = nc.tensor.transpose(self.psT[:, k * 128:(k + 1) * 128], self.xn[:, b.buf(2), k * CH:(k + 1) * CH], self.ident[:, :])
        last.then_inc(q["xt"], 1)

    def gain(self, act, b):
        nc, q = self.nc, self.q
        act.wait_ge(q["xt"], b.n + 1)
        if b.reached(2):
            act.wait_ge(q["up"], b.n - 1)
        for k in range(KC):
            last = nc.scalar.activation(self.h[:, b.buf(2), k, :], self.psT[:, k * 128:(k + 1) * 128], ACT.Identity,
                                        bias=self.gb[:, 1, k:k + 1], scale=self.gb[:, 0, k:k + 1])
        last.then_inc(q["h_ready"], 1)

    def up(self, pe, b):
        nc, q = self.nc, self.q
        pe.wait_ge(q["h_ready"], b.n + 1)
        if b.reached(2):
            pe.wait_ge(q["hid_ready"], b.n - 1)
        for m in range(MC):
            for k in range(KC):
                last = nc.tensor.matmul(self.psU[b.buf(2)][:, m * 128:(m + 1) * 128], self.w1[:, k, m * 128:(m + 1) * 128],
                                        self.h[:, b.buf(2), k, :], start=(k == 0), stop=(k == KC - 1))
        last.then_inc(q["up"], 1)

    def gelu(self, act, b, dims, dst_dims):
        nc, q = self.nc, self.q
        act.wait_ge(q["up"], b.n + 1)
        for m in range(MC):
            last = nc.scalar.activation(view(self.hid[:, b.buf(self.hring), m, 0:1], dst_dims), view(self.psU[b.buf(2)][:, m * 128:m * 128 + 1], dims),
                                        ACT.Gelu, bias=self.b1[:, m:m + 1])
        last.then_inc(q["hid_ready"], 1)


def mlp(nc, a, d, X, PS, stack):
    s = Scope(nc, "mlp", stack)
    n = NormUp(nc, s, X, PS, 1e-5, 2)
    w2 = s.sb("w2", [128, MC, C])
    b2 = s.sb("b2", [128, C])
    ab = s.sb("ab", [128, 2, C])
    x1 = s.sb("x1", [128, 2, C])
    strip = s.sb("strip", [CH, 2, KC, 8, HW])
    psD = [PS[:, 6 + i, 0:C] for i in range(2)]
    psT1 = PS[0:CH, 5, 0:256]
    q = {x: s.sem(x) for x in ("w2loaded", "ab_ready", "down", "x1_ready", "kept", "x1t", "strip_ready")}
    stored = s.sems("stored", 2)
    U, HEAD, LAG = 14, 14, 6

    with nc.Block() as block:
        @block.sync
        def _(sp):
            n.load(sp, a["L0_conv_fc1_w"], a["L0_conv_fc1_b"], a["L0_conv_ln2_g"], a["L0_conv_ln2_b"])
            sp.dma_start(w2[:, :, :], a["L0_conv_fc2_w"].rearrange("(m p) n -> p m n", m=MC)).then_inc(q["w2loaded"], 16)
            sp.dma_start(b2[:, :], a["L0_conv_fc2_b"].partition_broadcast(128)).then_inc(q["w2loaded"], 16)
            for img in range(IMG):
                with sp.Fori(0, BY // 2) as g:
                    for j in range(2):
                        t = g * 2 + (j + img * BY)
                        sp.wait_ge(q["strip_ready"], t * BX + BX)
                        sp.dma_start(d["x1"][img, :, bass.ds(g * 16 + (8 * j + 1), 8), :].rearrange("(k p) r x -> p k (r x)", k=KC),
                                     strip[:, j, :, :, :].rearrange("p k r x -> p k (r x)")).then_inc(stored[j], 16)
            for j in range(2):
                sp.wait_ge(stored[j], 16 * (NS // 2))

        @block.gpsimd
        def _(pool):
            n.constants(pool)
            pool.wait_ge(q["w2loaded"], 32)

            def body(t):
                b = t
                if b.inside(NB):
                    n.rstd(pool, b)
                b = t.back(4)
                if b.inside(NB):
                    if b.reached(2):
                        pool.wait_ge(q["x1_ready"], b.n - 1)
                    nc.gpsimd.tensor_tensor(ab[:, b.buf(2), :], at(X, b.n), b2[:, :], ALU.add).then_inc(q["ab_ready"], 1)
                b = t.back(6)
                if b.inside(NB):
                    reached = at_hand(pool, b.n + 1)
                    pool.wait_ge(q["w2loaded"], 32)
                    pool.wait_ge(q["x1_ready"], reached)
                    nc.gpsimd.tensor_copy(at(X, b.n), x1[:, b.buf(2), :]).then_inc(q["kept"], 1)
            run_steps(pool, NB, U, HEAD, LAG, body)

        @block.vector
        def _(dve):
            def body(t):
                b = t.back(1)
                if b.inside(NB):
                    n.normalize(dve, b)
                if t.inside(NB):
                    n.stats(dve, t)
                b = t.back(5)
                if b.inside(NB):
                    dve.wait_ge(q["down"], b.n + 1)
                    dve.wait_ge(q["ab_ready"], b.n + 1)
                    if b.reached(2):
                        dve.wait_ge(q["x1t"], b.n - 1)
                        dve.wait_ge(q["kept"], b.n - 1)
                    nc.vector.tensor_tensor(x1[:, b.buf(2), :], psD[b.buf(2)], ab[:, b.buf(2), :], ALU.add).then_inc(q["x1_ready"], 1)
            run_steps(dve, NB, U, HEAD, LAG, body)

        @block.scalar
        def _(act):
            n.wait_weights(act)

            def body(t):
                b = t.back(6)
                if b.inside(NB):
                    act.wait_ge(q["x1t"], b.n + 1)
                    if b.reached(2 * BX) and b.buf(BX) == 0:
                        act.wait_ge(stored[b.buf(2 * BX) // BX], b.turn(2 * BX) * 16)
                    for k in range(KC):
                        dst = strip[:, b.buf(2 * BX) // BX, k, :, b.buf(BX) * 16:b.buf(BX) * 16 + 16].rearrange("p r (w c) -> p w r c", w=2)
                        last = nc.scalar.activation(dst, psT1[:, k * 128:(k + 1) * 128].rearrange("p (w r c) -> p w r c", w=2, r=8), ACT.Identity)
                    last.then_inc(q["strip_ready"], 1)
                b = t.back(2)
                if b.inside(NB):
                    n.gain(act, b)
                b = t.back(3)
                if b.inside(NB):
                    if b.reached(2):
                        act.wait_ge(q["down"], b.n - 1)
                    n.gelu(act, b, [[1, 128]], [[1, 128]])
            run_steps(act, NB, U, HEAD, LAG, body)

        @block.tensor
        def _(pe):
            n.wait_weights(pe)
            pe.wait_ge(q["w2loaded"], 32)

            def body(t):
                b = t.back(6)
                if b.inside(NB):
                    pe.wait_ge(q["x1_ready"], b.n + 1)
                    if b.reached(1):
                        pe.wait_ge(q["strip_ready"], b.n)
                    for k in range(KC):
                        last = nc.tensor.transpose(psT1[:, k * 128:(k + 1) * 128], x1[:, b.buf(2), k * CH:(k + 1) * CH], n.ident[:, :])
                    last.then_inc(q["x1t"], 1)
                b = t.back(2)
                if b.inside(NB):
                    n.transpose(pe, b)
                b = t.back(5)
                if b.inside(NB):
                    pe.wait_ge(n.q["hid_ready"], b.n + 1)
                    if b.reached(2):
                        pe.wait_ge(q["x1_ready"], b.n - 1)
                    for m in range(MC):
                        last = nc.tensor.matmul(psD[b.buf(2)], n.hid[:, b.buf(2), m, :], w2[:, m, :], start=(m == 0), stop=(m == MC - 1))
                    last.then_inc(q["down"], 1)
                b = t.back(3)
                if b.inside(NB):
                    n.up(pe, b)
            run_steps(pe, NB, U, HEAD, LAG, body)


def sobel(nc, a, d, X, PS, stack):
    s = Scope(nc, "sobel", stack)
    wf = s.sb("wf", [CH + 1, 2 * KC, C])
    row = s.sb("row", [128, 2, C])
    xin = s.sb("xin", [CH, KC, 10, HW + 2])
    down = s.sb("down", [CH, 8, HW + 2])
    diff = s.sb("diff", [CH, 8, HW + 2])
    half = s.sb("half", [CH, 8, HW + 1])
    edge = s.sb("edge", [CH + 1, 2, 2 * KC, BX, 128])
    f = s.sb("f", [128, BX, C])
    st = s.sb("st", [128, BX, 6])
    mv = s.sb("mv", [128, BX, 2])
    ve = s.sb("ve", [128, BX])
    rs = s.sb("rs", [128, BX])
    nb = s.sb("nb", [128, BX])
    small = s.sb("small", [128, 2, BX])
    loaded = s.sems("loaded", KC)
    q = {x: s.sem(x) for x in ("wloaded", "ready", "down1", "down2", "ex", "diff", "half", "ey", "fused", "stats", "aggr", "var_ok",
                               "rstd", "shift", "normed", "scaled", "affine", "gelu", "added", "stored")}
    U, HEAD, LAG = 2, 4, 3
    SLAG = 4
    READY = 4

    def psF(t, j):
        return PS[:, 4 * t.buf(2) + j // 2, j % 2 * 256:j % 2 * 256 + C]

    def in_blocks(t, e):
        return view(edge[0:CH, t.buf(2), e, 0, 0:1], [[8, 8], [64, 2 * BX], [1, 8]])

    def per_block(i):
        return view(row[:, i, 0:1], [[0, BX], [1, C]])

    def rows8(ap):
        return ap.rearrange("p r (b c) -> p r b c", c=8)

    with nc.Block() as block:
        @block.sync
        def _(sp):
            sp.dma_start(wf[0:CH, :, :], a["L1_conv_fusion_wT"].rearrange("(k p) n -> p k n", p=CH)).then_inc(q["wloaded"], 16)
            sp.dma_start(wf[CH:CH + 1, 0, :], a["L1_conv_fusion_b"].partition_broadcast(1)).then_inc(q["wloaded"], 16)
            for i, name in enumerate(("ln_w", "ln_b")):
                sp.dma_start(row[:, i, :], a["L1_conv_" + name].partition_broadcast(128)).then_inc(q["wloaded"], 16)
            sp.wait_ge(q["ready"], READY)

            def load(t, img, r):
                for k in range(KC):
                    if t.reached(1):
                        sp.wait_ge(q["down2"], t.n * KC + k - KC + 1)
                        sp.wait_ge(q["diff"], t.n * KC + k - KC + 1)
                    sp.dma_start(xin[:, k, :, 1:HW + 1], d["x1"][img, k * CH:(k + 1) * CH, r, :]).then_inc(loaded[k], 16)

            def store(t):
                sp.wait_ge(q["added"], t.n + 1)
                sp.dma_start(d["x2"][bass.ds(t.n * BX, BX)].rearrange("b p c -> p b c"), X[:, bass.ds(t.n * BX, BX), :]).then_inc(q["stored"], 16)

            for img in range(IMG):
                for j in range(SLAG):
                    t = Step(0, img * BY + j, 1)
                    load(t, img, slice(8 * j, 8 * j + 10))
                    if t.reached(SLAG):
                        store(t.back(SLAG))
                with sp.Fori(SLAG, BY) as g:
                    load(Step(g, img * BY, 1), img, bass.ds(g * 8, 10))
                    store(Step(g, img * BY - SLAG, 1))
            for j in range(NS - SLAG, NS):
                store(Step(0, j, 1))
            sp.wait_ge(q["stored"], 16 * NS)

        @block.gpsimd
        def _(pool):
            for i, (where, what) in enumerate(((xin[:, :, :, 0:HW + 2:HW + 1], 0.0), (edge[CH:CH + 1, :, 0, :, :], 1.0),
                                               (small[:, 0, :], 1e-5), (small[:, 1, :], -0.5))):
                nc.gpsimd.memset(where, what).then_inc(q["ready"], 1)
                pool.wait_ge(q["ready"], i + 1)

            def edge_y(t, k):
                b = t.n * KC + k
                pool.wait_ge(loaded[k], t.n * 16 + 16)
                if t.reached(1) or k:
                    pool.wait_ge(q["half"], b)
                nc.gpsimd.tensor_tensor(diff[:, :, :], xin[:, k, 2:10, :], xin[:, k, 0:8, :], ALU.subtract).then_inc(q["diff"], 1)
                pool.wait_ge(q["diff"], b + 1)
                if t.reached(1) or k:
                    pool.wait_ge(q["ey"], b)
                nc.gpsimd.tensor_tensor(half[:, :, :], diff[:, :, 1:HW + 2], diff[:, :, 0:HW + 1], ALU.add).then_inc(q["half"], 1)
                pool.wait_ge(q["half"], b + 1)
                if t.reached(2):
                    pool.wait_ge(q["fused"], t.n * BX - BX)
                nc.gpsimd.tensor_tensor(in_blocks(t, KC + k), rows8(half[:, :, 1:HW + 1]), rows8(half[:, :, 0:HW]), ALU.add).then_inc(q["ey"], 1)

            def body(t):
                if t.inside(NS):
                    edge_y(t, 0)
                b = t.back(2)
                if b.inside(NS):
                    pool.wait_ge(q["aggr"], b.n * BX + BX)
                    if b.reached(1):
                        pool.wait_ge(q["rstd"], b.n)
                    nc.gpsimd.tensor_tensor(ve[:, :], mv[:, :, 1], small[:, 0, :], ALU.add).then_inc(q["var_ok"], 1)
                    pool.wait_ge(q["var_ok"], b.n + 1)
                    if b.reached(1):
                        pool.wait_ge(q["normed"], b.n * BX)
                    nc.gpsimd.tensor_tensor(rs[:, :], ve[:, :], small[:, 1, :], ALU.pow).then_inc(q["rstd"], 1)
                    pool.wait_ge(q["rstd"], b.n + 1)
                if t.inside(NS):
                    edge_y(t, 1)
            run_steps(pool, NS, U, HEAD, LAG, body)

        @block.vector
        def _(dve):
            dve.wait_ge(q["ready"], READY)
            dve.wait_ge(q["wloaded"], 64)

            def edge_x(t, k):
                b = t.n * KC + k
                dve.wait_ge(loaded[k], t.n * 16 + 16)
                if t.reached(1) or k:
                    dve.wait_ge(q["ex"], b)
                nc.vector.scalar_tensor_tensor(down[:, :, :], xin[:, k, 1:9, :], 2.0, xin[:, k, 0:8, :], ALU.mult, ALU.add).then_inc(q["down1"], 1)
                dve.wait_ge(q["down1"], b + 1)
                nc.vector.tensor_tensor(down[:, :, :], down[:, :, :], xin[:, k, 2:10, :], ALU.add).then_inc(q["down2"], 1)
                dve.wait_ge(q["down2"], b + 1)
                if t.reached(2):
                    dve.wait_ge(q["fused"], t.n * BX - BX)
                nc.vector.tensor_tensor(in_blocks(t, k), rows8(down[:, :, 2:HW + 2]), rows8(down[:, :, 0:HW]), ALU.subtract).then_inc(q["ex"], 1)

            def body(t):
                b = t.back(3)
                if b.inside(NS):
                    dve.wait_ge(q["gelu"], b.n + 1)
                    strip = X[:, bass.ds(b.n * BX, BX), :]
                    nc.vector.tensor_tensor(strip, strip, f[:, :, :], ALU.add).then_inc(q["added"], 1)
                b = t.back(2)
                if b.inside(NS):
                    if b.reached(1):
                        dve.wait_ge(q["aggr"], b.n * BX)
                    for j in range(BX):
                        if j % 2 == 0:
                            dve.wait_ge(q["fused"], b.n * BX + min(j + 2, BX))
                        nc.vector.bn_stats(out=st[:, j, :], in_=psF(b, j)).then_inc(q["stats"], 1)
                    if b.reached(1):
                        dve.wait_ge(q["shift"], b.n)
                        dve.wait_ge(q["var_ok"], b.n)
                    for j in range(BX):
                        reached = at_hand(dve, b.n * BX + j + 1)
                        dve.wait_ge(q["ready"], READY)
                        dve.wait_ge(q["stats"], reached)
                        nc.vector.bn_aggr(out=mv[:, j, :], in_=st[:, j, :]).then_inc(q["aggr"], 1)
                if t.inside(NS):
                    edge_x(t, 0)
                if b.inside(NS):
                    dve.wait_ge(q["rstd"], b.n + 1)
                    dve.wait_ge(q["aggr"], b.n * BX + BX)
                    if b.reached(1):
                        dve.wait_ge(q["normed"], b.n * BX)
                    nc.vector.scalar_tensor_tensor(nb[:, :], mv[:, :, 0], -1.0, rs[:, :], ALU.mult, ALU.mult).then_inc(q["shift"], 1)
                if t.inside(NS):
                    edge_x(t, 1)
                if b.inside(NS):
                    dve.wait_ge(q["normed"], b.n * BX + BX)
                    nc.vector.tensor_tensor(f[:, :, :], f[:, :, :], per_block(0), ALU.mult).then_inc(q["scaled"], 1)
                    dve.wait_ge(q["scaled"], b.n + 1)
                    nc.vector.tensor_tensor(f[:, :, :], f[:, :, :], per_block(1), ALU.add).then_inc(q["affine"], 1)
            run_steps(dve, NS, U, HEAD, LAG, body)

        @block.scalar
        def _(act):
            def body(t):
                b = t.back(2)
                if b.inside(NS):
                    act.wait_ge(q["shift"], b.n + 1)
                    act.wait_ge(q["rstd"], b.n + 1)
                    if b.reached(1):
                        act.wait_ge(q["added"], b.n)
                    for j in range(BX):
                        nc.scalar.activation(f[:, j, :], psF(b, j), ACT.Identity, bias=nb[:, j:j + 1], scale=rs[:, j:j + 1]).then_inc(q["normed"], 1)
                    act.wait_ge(q["affine"], b.n + 1)
                    nc.scalar.activation(f[:, :, :], f[:, :, :], ACT.Gelu).then_inc(q["gelu"], 1)
            run_steps(act, NS, U, HEAD, 2, body)

        @block.tensor
        def _(pe):
            pe.wait_ge(q["wloaded"], 64)
            pe.wait_ge(q["ready"], READY)

            def body(t):
                pe.wait_ge(q["ex"], t.n * KC + KC)
                pe.wait_ge(q["ey"], t.n * KC + KC)
                if t.reached(2):
                    pe.wait_ge(q["normed"], t.n * BX - BX)
                for j in range(BX):
                    for e in range(2 * KC):
                        rows = CH + 1 if e == 0 else CH
                        last = nc.tensor.matmul(psF(t, j), edge[0:rows, t.buf(2), e, j, :], wf[0:rows, e, :], start=(e == 0), stop=(e == 2 * KC - 1))
                    last.then_inc(q["fused"], 1)
            run_steps(pe, NS, U, HEAD, 0, body)


def depthwise(nc, tag, taps, bias, X, PS, out, stack):
    s = Scope(nc, tag, stack)
    U, HEAD, LAG, R = 4, 8, 2, 2
    raw = s.sb("raw", [128, U, GRUN])
    mats = s.sb("mats", [128, R, 2, 24, 16])
    xc = s.sb("xc", [128, R, IMG, BY, BX])
    xs = s.sb("xs", [128, R, IMG * BY, BX])
    brow = s.sb("brow", [128, C])
    res = s.sb("res", [128, 2, U, NB]) if out is not None else None
    loaded = s.sems("loaded", U)
    q = {x: s.sem(x) for x in ("bloaded", "ready", "mats_a", "mats_b", "xc_ready", "xs_half", "xs_ready", "conv", "result")}
    stored = s.sems("stored", 2)

    def ps(b):
        return PS[:, b.buf(4), 0:NB].rearrange("p (i y x) -> p i y x", i=IMG, y=BY)

    def toeplitz(b, shifted):
        return view(raw[:, b.buf(U), 0:1], [[-GP, 24], [-1, 16]], 23 * GP + 15 + 16 * shifted)

    with nc.Block() as block:
        @block.sync
        def _(sp):
            sp.dma_start(brow[:, :], bias.partition_broadcast(128)).then_inc(q["bloaded"], 16)

            def body(t):
                b = t
                if b.reached(U):
                    sp.wait_ge(q["mats_a"], b.n - U + 1)
                    sp.wait_ge(q["mats_b"], b.n - U + 1)
                for h in range(2):
                    src = bass.AP(taps.tensor, taps.offset + h * C * GSZ + b.n * GSZ, [[GP, 8], [1, 8], [1, GRUN]])
                    sp.dma_start(raw[64 * h:64 * h + 64, b.buf(U), :], src).then_inc(loaded[b.buf(U)], 16)
            run_steps(sp, C, U, HEAD, 0, body)

        @block.gpsimd
        def _(pool):
            nc.gpsimd.memset(xs[:, :, :, :], 0.0).then_inc(q["ready"], 1)
            pool.wait_ge(q["ready"], 1)

            def body(t):
                b = t
                reached = at_hand(pool, b.n - R + 1)
                pool.wait_ge(q["ready"], 1)
                if b.reached(R):
                    pool.wait_ge(q["conv"], reached)
                for h in range(2):
                    if h:
                        pool.wait_ge(q["xs_half"], b.n + 1)
                    src = X[64 * h:64 * h + 64, :, bass.ds(b.n, 1)].rearrange("p (y x) o -> p y (x o)", x=BX)
                    dst = xs[64 * h:64 * h + 64, b.buf(R), :, :]
                    last = nc.gpsimd.tensor_copy(dst[:, :, h:h + BX - 1], src[:, :, 1 - h:BX - h])
                    if not h:
                        last.then_inc(q["xs_half"], 1)
                last.then_inc(q["xs_ready"], 1)
            run_steps(pool, C, U, HEAD, 0, body)

        @block.vector
        def _(dve):
            def body(t):
                b = t
                if b.reached(R):
                    dve.wait_ge(q["conv"], b.n - R + 1)
                nc.vector.tensor_copy(xc[:, b.buf(R)].rearrange("p i y x -> p (i y x)"), X[:, :, bass.ds(b.n, 1)].rearrange("p b o -> p (b o)"))\
                    .then_inc(q["xc_ready"], 1)
                dve.wait_ge(loaded[b.buf(U)], b.turn(U) * 32 + 32)
                nc.vector.tensor_copy(mats[:, b.buf(R), 0], toeplitz(b, 0)).then_inc(q["mats_a"], 1)
            run_steps(dve, C, U, HEAD, 0, body)

        @block.scalar
        def _(act):
            act.wait_ge(q["bloaded"], 16)

            def body(t):
                b = t
                if b.inside(C):
                    if b.reached(R):
                        act.wait_ge(q["conv"], b.n - R + 1)
                    act.wait_ge(loaded[b.buf(U)], b.turn(U) * 32 + 32)
                    nc.scalar.activation(mats[:, b.buf(R), 1], toeplitz(b, 1), ACT.Identity).then_inc(q["mats_b"], 1)
                b = t.back(2)
                if b.inside(C):
                    act.wait_ge(q["conv"], b.n + 1)
                    src = PS[:, b.buf(4), 0:NB]
                    if out is None:
                        dst = X[:, :, bass.ds(b.n, 1)].rearrange("p b o -> p (b o)")
                    else:
                        dst = res[:, b.buf(2 * U) // U, b.buf(U), :]
                        if b.reached(2 * U) and b.buf(U) == 0:
                            act.wait_ge(stored[b.buf(2 * U) // U], b.turn(2 * U) * 16)
                    nc.scalar.activation(dst, src, ACT.Identity, bias=brow[:, bass.ds(b.n, 1)]).then_inc(q["result"], 1)
                    if out is not None and b.buf(U) == U - 1:
                        act.wait_ge(q["result"], b.n + 1)
                        act.dma_start(out[bass.ds(b.n - (U - 1), U)].rearrange("c p b -> p c b"), res[:, b.buf(2 * U) // U]).then_inc(stored[b.buf(2 * U) // U], 16)
            run_steps(act, C, 2 * U, HEAD, LAG, body)
            if out is not None:
                for j in range(2):
                    act.wait_ge(stored[j], 16 * (C // U // 2))

        @block.tensor
        def _(pe):
            def body(t):
                b = t
                pe.wait_ge(q["xc_ready"], b.n + 1)
                pe.wait_ge(q["xs_ready"], b.n + 1)
                pe.wait_ge(q["mats_a"], b.n + 1)
                pe.wait_ge(q["mats_b"], b.n + 1)
                if b.reached(4):
                    pe.wait_ge(q["result"], b.n - 3)
                src = (xc[:, b.buf(R)], xs[:, b.buf(R)].rearrange("p (i y) x -> p i y x", i=IMG))
                for i, (oy, sh) in enumerate(((0, 0), (0, 1), (-1, 0), (-1, 1), (1, 0), (1, 1))):
                    ylo, yhi = max(0, -oy), BY - max(0, oy)
                    m = mats[:, b.buf(R), sh, 8 * (1 - oy):8 * (1 - oy) + 8, :].rearrange("p r c -> p (r c)")
                    last = nc.tensor.matmul(ps(b)[:, :, ylo:yhi, :], m, src[sh][:, :, ylo + oy:yhi + oy, :], start=(i == 0), stop=(i == 5))
                last.then_inc(q["conv"], 1)
            run_steps(pe, C, U, HEAD, 0, body)


def hidden(nc, a, d, X, PS, gain2, cvec, stack):
    s = Scope(nc, "hid", stack)
    HR = 4
    n = NormUp(nc, s, X, PS, 1e-6, HR)
    sq = s.sb("sq", [128, 2, MC, 128])
    ss = s.sb("ss", [128, NB, MC])
    q = {x: s.sem(x) for x in ("sq", "ss")}
    stored = s.sems("stored", HR)
    U, HEAD, LAG = 4, 8, 4

    with nc.Block() as block:
        @block.sync
        def _(sp):
            n.load(sp, a["L2_conv_w1"], a["L2_conv_b1"], a["L2_conv_ln_w"], a["L2_conv_ln_b"])

            def body(b):
                sp.wait_ge(n.q["hid_ready"], b.n + 1)
                sp.dma_start(d["hid"][bass.ds(b.n, 1)].rearrange("o p m t -> (o p) m t"), n.hid[:, b.buf(HR), :, :]).then_inc(stored[b.buf(HR)], 16)
            run_steps(sp, NB, U, HEAD, 0, body)
            for j in range(HR):
                sp.wait_ge(stored[j], 16 * (NB // HR))

        @block.gpsimd
        def _(pool):
            n.constants(pool)

            def body(t):
                if t.inside(NB):
                    n.rstd(pool, t)
                b = t.back(3)
                if b.inside(NB):
                    pool.wait_ge(n.q["hid_ready"], b.n + 1)
                    if b.reached(2):
                        pool.wait_ge(q["ss"], b.n - 1)
                    hb = n.hid[:, b.buf(HR), :, :]
                    nc.gpsimd.tensor_tensor(sq[:, b.buf(2)], hb, hb, ALU.mult).then_inc(q["sq"], 1)
            run_steps(pool, NB, U, HEAD, LAG, body)

        @block.vector
        def _(dve):
            def body(t):
                b = t.back(1)
                if b.inside(NB):
                    n.normalize(dve, b)
                if t.inside(NB):
                    n.stats(dve, t)
                b = t.back(4)
                if b.inside(NB):
                    dve.wait_ge(q["sq"], b.n + 1)
                    nc.vector.reduce_sum(at(ss, b.n), sq[:, b.buf(2)], AX.X).then_inc(q["ss"], 1)
            run_steps(dve, NB, U, HEAD, LAG, body)

        @block.scalar
        def _(act):
            n.wait_weights(act)

            def body(t):
                b = t.back(2)
                if b.inside(NB):
                    n.gain(act, b)
                b = t.back(3)
                if b.inside(NB):
                    if b.reached(HR):
                        act.wait_ge(stored[b.buf(HR)], b.turn(HR) * 16)
                        act.wait_ge(q["sq"], b.n - HR + 1)
                    n.gelu(act, b, [[16, 8], [8, 2], [1, 8]], [[8, 8], [64, 2], [1, 8]])
            run_steps(act, NB, U, HEAD, LAG, body)

        @block.tensor
        def _(pe):
            n.wait_weights(pe)

            def body(t):
                b = t.back(2)
                if b.inside(NB):
                    n.transpose(pe, b)
                b = t.back(3)
                if b.inside(NB):
                    n.up(pe, b)
            run_steps(pe, NB, U, HEAD, LAG, body)

    w2 = s.sb("w2", [128, MC, C])
    gbv = s.sb("gbv", [128, 2, MC])
    beta = s.sb("beta", [128, MC, 128])
    b2 = s.sb("b2", [128, C])
    ones = s.sb("ones", [128, 128])
    phalf = s.sb("phalf", [128, IMG, MC])
    tot = s.sb("tot", [128, IMG, MC])
    gx = s.sb("gx", [128, IMG, MC])
    mean = s.sb("mean", [128, IMG])
    scale = s.sb("scale", [128, IMG, MC])
    psM = PS[:, 0, 0:IMG * MC]
    psC = PS[:, 1, 0:C]
    g = {x: s.sem("grn_" + x) for x in ("loaded", "ready", "tot", "gx", "sums", "chain", "beta", "const")}
    with nc.Block() as block:
        @block.sync
        def _(sp):
            sp.dma_start(w2[:, :, :], a["L2_conv_w2"].rearrange("(m p) n -> p m n", m=MC)).then_inc(g["loaded"], 16)
            sp.dma_start(gbv[:, 0, :], a["L2_conv_grn_gamma"].rearrange("(m p) -> p m", m=MC)).then_inc(g["loaded"], 16)
            sp.dma_start(gbv[:, 1, :], a["L2_conv_grn_beta"].rearrange("(m p) -> p m", m=MC)).then_inc(g["loaded"], 16)
            sp.dma_start(b2[:, :], a["L2_conv_b2"].partition_broadcast(128)).then_inc(g["loaded"], 16)

        @block.gpsimd
        def _(pool):
            nc.gpsimd.memset(ones[:, :], 1.0).then_inc(g["ready"], 1)
            nc.gpsimd.memset(phalf[:, :, :], 0.5).then_inc(g["ready"], 1)
            pool.wait_ge(g["ready"], 2)
            pool.wait_ge(g["tot"], 1)
            nc.gpsimd.tensor_tensor(gx[:, :, :], tot[:, :, :], phalf[:, :, :], ALU.pow).then_inc(g["gx"], 1)

        @block.tensor
        def _(pe):
            pe.wait_ge(g["gx"], 1)
            nc.tensor.matmul(psM, ones[:, :], gx[:, :, :].rearrange("p i m -> p (i m)"), start=True, stop=True).then_inc(g["sums"], 1)
            pe.wait_ge(g["loaded"], 64)
            pe.wait_ge(g["beta"], 1)
            for m in range(MC):
                last = nc.tensor.matmul(psC, beta[:, m, :], w2[:, m, :], start=(m == 0), stop=(m == MC - 1))
            last.then_inc(g["const"], 1)

        @block.vector
        def _(dve):
            done = [0]

            def then(ins):
                done[0] += 1
                ins.then_inc(g["chain"], 1)
                dve.wait_ge(g["chain"], done[0])

            nc.vector.reduce_sum(tot[:, :, :], ss[:, :, :].rearrange("p (i n) m -> p i m n", i=IMG), AX.X).then_inc(g["tot"], 1)
            dve.wait_ge(g["loaded"], 64)
            nc.vector.tensor_copy(beta[:, :, :], view(gbv[:, 1, 0:1], [[1, MC], [0, 128]])).then_inc(g["beta"], 1)
            dve.wait_ge(g["sums"], 1)
            then(nc.vector.reduce_sum(mean[:, :], psM.rearrange("p (i m) -> p i m", i=IMG), AX.X))
            then(nc.vector.tensor_scalar(mean[:, :], mean[:, :], 1.0 / HID, 1e-6, ALU.mult, ALU.add))
            then(nc.vector.reciprocal(mean[:, :], mean[:, :]))
            for i in range(IMG):
                then(nc.vector.scalar_tensor_tensor(scale[:, i, :], gx[:, i, :], mean[:, i:i + 1], gbv[:, 0, :], ALU.mult, ALU.mult))
            then(nc.vector.tensor_scalar(scale[:, :, :], scale[:, :, :], 1.0, None, ALU.add))
            for i in range(IMG):
                for m in range(MC):
                    nc.vector.tensor_scalar(gain2[:, i, m, :], w2[:, m, :], scale[:, i, m:m + 1], None, ALU.mult)
            dve.wait_ge(g["const"], 1)
            nc.vector.tensor_tensor(cvec[:, :], psC, b2[:, :], ALU.add)


def project(nc, a, d, X, PS, gain2, cvec, stack):
    s = Scope(nc, "down", stack)
    R = BX
    hid = s.sb("hid", [128, R, MC, 128])
    x2 = s.sb("x2", [128, R, C])
    hloaded, xloaded = s.sems("hloaded", R), s.sems("xloaded", R)
    q = {x: s.sem(x) for x in ("resid", "down", "out")}
    with nc.Block() as block:
        @block.sync
        def _(sp):
            def body(b):
                if b.reached(R):
                    sp.wait_ge(q["down"], b.n - R + 1)
                sp.dma_start(hid[:, b.buf(R)], d["hid"][bass.ds(b.n, 1)].rearrange("o p m t -> (o p) m t")).then_inc(hloaded[b.buf(R)], 16)
                if b.reached(R):
                    sp.wait_ge(q["out"], b.n - R + 1)
                sp.dma_start(x2[:, b.buf(R), :], d["x2"][bass.ds(b.n, 1)].rearrange("o p c -> (o p) c")).then_inc(xloaded[b.buf(R)], 16)
            run_steps(sp, NB, R, R, 0, body)

        @block.gpsimd
        def _(pool):
            def body(b):
                pool.wait_ge(xloaded[b.buf(R)], b.turn(R) * 16 + 16)
                nc.gpsimd.tensor_tensor(x2[:, b.buf(R), :], x2[:, b.buf(R), :], cvec[:, :], ALU.add).then_inc(q["resid"], 1)
            run_steps(pool, NB, R, R, 0, body)

        @block.vector
        def _(dve):
            def body(b):
                dve.wait_ge(q["resid"], b.n + 1)
                dve.wait_ge(q["down"], b.n + 1)
                nc.vector.tensor_tensor(at(X, b.n), PS[:, b.buf(R), 0:C], x2[:, b.buf(R), :], ALU.add).then_inc(q["out"], 1)
            run_steps(dve, NB, R, R, 0, body)

        @block.tensor
        def _(pe):
            for img in range(IMG):
                def body(b):
                    b = Step(b.g, b.j + img * PER, R)
                    pe.wait_ge(hloaded[b.buf(R)], b.turn(R) * 16 + 16)
                    if b.reached(R):
                        pe.wait_ge(q["out"], b.n - R + 1)
                    for m in range(MC):
                        last = nc.tensor.matmul(PS[:, b.buf(R), 0:C], hid[:, b.buf(R), m, :], gain2[:, img, m, :], start=(m == 0), stop=(m == MC - 1))
                    last.then_inc(q["down"], 1)
                run_steps(pe, PER, R, R, 0, body)


def build(nc, a, out):
    d = {"x": a["x"]}
    d["x1"] = nc.dram_tensor("scratch_x1", [IMG, C, HW + 2, HW], F32, kind="Internal").ap()
    d["x2"] = nc.dram_tensor("scratch_x2", [NB, 128, C], F32, kind="Internal").ap()
    d["hid"] = nc.dram_tensor("scratch_hid", [NB, 128, MC, 128], F32, kind="Internal").ap()
    d["taps"] = nc.dram_tensor("scratch_taps", [2, 2, C, GSZ], F32, kind="Internal").ap()
    d["bias"] = nc.dram_tensor("scratch_bias", [C], F32, kind="Internal").ap()
    with ExitStack() as stack:
        stack.enter_context(nc.allow_non_contiguous_dma(reason="vectors of 192 to 768 elements, once"))
        prepare(nc, a, d, stack)
    with ExitStack() as whole:
        whole.enter_context(nc.allow_non_contiguous_dma(reason="vectors of 192 to 768 elements, once"))
        X = whole.enter_context(nc.sbuf_tensor("X", [128, NB, C], F32))
        PS = whole.enter_context(nc.psum_tensor("PS", [128, 8, 512], F32))
        with ExitStack() as stack:
            attention(nc, a, d, X, PS, stack)
        with ExitStack() as stack:
            mlp(nc, a, d, X, PS, stack)
        with ExitStack() as stack:
            sobel(nc, a, d, X, PS, stack)
        with ExitStack() as stack:
            depthwise(nc, "dw7", d["taps"][0], a["L2_conv_dw_b"], X, PS, None, stack)
        with ExitStack() as both:
            gain2 = both.enter_context(nc.sbuf_tensor("gain2", [128, IMG, MC, C], F32))
            cvec = both.enter_context(nc.sbuf_tensor("cvec", [128, C], F32))
            with ExitStack() as stack:
                hidden(nc, a, d, X, PS, gain2, cvec, stack)
            with ExitStack() as stack:
                project(nc, a, d, X, PS, gain2, cvec, stack)
        with ExitStack() as stack:
            depthwise(nc, "dw13", d["taps"][1], d["bias"], X, PS, out, stack)


def kernel(**inputs):
    import numpy as np
    import concourse.bacc as bacc
    from concourse.bass_utils import run_bass_kernel_spmd

    nc = bacc.Bacc("TRN2", target_bir_lowering=False, num_devices=1)
    arrays, a = {}, {}
    for name, v in inputs.items():
        v = np.asarray(v)
        if name == "x":
            v = v.reshape(IMG, C, BY, 8, BX, 2, 8).transpose(0, 2, 4, 5, 3, 6, 1).reshape(NB, 128, C)
        if name == "L1_conv_fusion_w":
            name, v = "L1_conv_fusion_wT", v.T
        if "conv_bn_" in name:
            v = v.T
        v = np.ascontiguousarray(v)
        arrays["in_" + name] = v
        a[name] = nc.dram_tensor("in_" + name, v.shape, mybir.dt.from_np(v.dtype), kind="ExternalInput").ap()
    out = nc.dram_tensor("out", [C, 128, NB], F32, kind="ExternalOutput").ap()
    build(nc, a, out)
    r = run_bass_kernel_spmd(nc, [arrays], core_ids=[0])
    y = r.results[0]["out"].reshape(C, 8, 16, IMG, BY, BX)
    return np.ascontiguousarray(y.transpose(3, 0, 4, 1, 5, 2)).reshape(IMG, C, HW, HW)
```

```python
import concourse.bass as bass
from concourse import mybir
from contextlib import ExitStack

F32 = mybir.dt.float32
F32R = mybir.dt.float32r
ALU = mybir.AluOpType
ACT = mybir.ActivationFunctionType
AX = mybir.AxisListType

C = 192
KC = 2
CH = C // KC
HID = 4 * C
MC = HID // 128
IMG, BY, BX = 2, 14, 7
HW = 112
PER = BY * BX
NB = IMG * PER
NP = NB // 2
NS = IMG * BY
NH, HD = 8, 24
ROW = HW * 8

KW = 13
GP = 40
GROWS = 32
GSZ = GROWS * GP
GRUN = 24 * GP
GR0 = 9
GC0 = (9, 1)
GWRAP = 33
WRAPC = 6


class Step:

    def __init__(self, g, j, unroll):
        self.g, self.j, self.unroll = g, j, unroll

    def ahead(self, k):
        return Step(self.g, self.j + k, self.unroll)

    def blocks(self):
        return [Step(self.g, 2 * self.j + i, 2 * self.unroll) for i in range(2)]

    def back(self, lag):
        return Step(self.g, self.j - lag, self.unroll)

    @property
    def n(self):
        return self.g * self.unroll + self.j

    def upto(self, k):
        return min(self.n + k, NB) if self.fixed else self.n + k

    @property
    def fixed(self):
        return isinstance(self.g, int)

    def reached(self, k):
        return not self.fixed or self.n >= k

    def inside(self, count):
        return not self.fixed or 0 <= self.n < count

    def buf(self, ring):
        return self.j % ring

    def turn(self, ring):
        return self.g * (self.unroll // ring) + self.j // ring


def run_steps(eng, count, unroll, head, lag, body):
    assert (count - head) % unroll == 0
    for j in range(head):
        body(Step(0, j, unroll))
    with eng.Fori(0, (count - head) // unroll) as g:
        for j in range(unroll):
            body(Step(g, head + j, unroll))
    for j in range(count, count + lag):
        body(Step(0, j, unroll))


def at_hand(eng, value):
    return value if isinstance(value, int) else eng.snap(eng.to_reg(value))


def view(ap, dims, shift=0):
    return bass.AP(ap.tensor, ap.offset + shift, [list(ap.ap[0])] + [list(d) for d in dims])


def at(ap, i):
    return ap[:, bass.ds(i, 1)].rearrange("p o c -> p (o c)")


def as_f32(ap):
    return ap.bitcast(F32)


def product(nc, out, lhs, rhs, chunks):
    for c in range(chunks):
        (lh, ll), (rh, rl) = lhs(c), rhs(c)
        nc.tensor.matmul(out, lh, rh, start=(c == 0), stop=False)
        nc.tensor.matmul(out, lh, rl, start=False, stop=False)
        last = nc.tensor.matmul(out, ll, rh, start=False, stop=(c == chunks - 1))
    return last


class Scope:

    def __init__(self, nc, tag, stack):
        self.nc, self.tag, self.stack = nc, tag, stack

    def sb(self, name, shape, dtype=F32):
        return self.stack.enter_context(self.nc.sbuf_tensor(f"{self.tag}_{name}", shape, dtype))

    def parts(self, name, shape):
        return self.sb(name + "_hi", shape, F32R), self.sb(name + "_lo", shape, F32R)

    def sem(self, name):
        return self.nc.alloc_semaphore(f"{self.tag}_{name}")

    def sems(self, name, n):
        return [self.sem(f"{name}{i}") for i in range(n)]


def prepare(nc, a, d, stack):
    s = Scope(nc, "prep", stack)
    taps = ["w_lk", "w_b0", "w_b1", "w_b2", "w_b3", "w_b4", "w_b5"]
    dilation = [1, 1, 1, 2, 3, 4, 5]
    side = [13, 5, 7, 7, 3, 3, 3]
    wt = [s.sb(f"taps{i}", [CH, KC, k, k]) for i, k in enumerate(side)]
    w7 = s.sb("taps7", [CH, KC, 7, 7])
    bn = s.sb("bn", [CH, 4, KC, 7])
    merged = s.sb("merged", [CH, KC, KW, KW])
    inv = s.sb("inv", [CH, KC, 7])
    half = s.sb("half", [CH, KC, 7])
    shift = s.sb("shift", [CH, KC, 7])
    bias = s.sb("bias", [CH, KC])
    zrow = s.sb("zrow", [CH, KC, HW])
    padded = [[s.sb(f"pad{i}{h}", [CH, KC, GSZ]) for h in range(2)] for i in range(2)]
    loaded, var_ok, inv_ok, zeroed, built, biased, stored, chain, cleared = (
        s.sem(x) for x in ("loaded", "var_ok", "inv_ok", "zeroed", "built", "biased", "stored", "chain", "cleared"))
    nload = len(taps) + 1 + 4

    with nc.Block() as block:
        @block.sync
        def _(sp):
            for t, name in zip(wt, taps):
                sp.dma_start(t[:, :, :, :], a["L3_conv_" + name].rearrange("(k p) o y x -> p k (o y) x", k=KC)).then_inc(loaded, 16)
            sp.dma_start(w7[:, :, :, :], a["L2_conv_dw_w"].rearrange("(k p) o y x -> p k (o y) x", k=KC)).then_inc(loaded, 16)
            for i, name in enumerate(("gamma", "beta", "mean", "var")):
                sp.dma_start(bn[:, i, :, :], a["L3_conv_bn_" + name].rearrange("(k p) j -> p k j", k=KC)).then_inc(loaded, 16)
            sp.wait_ge(zeroed, 1)
            for img in range(IMG):
                for r in (0, HW + 1):
                    sp.dma_start(d["x1"][img, :, r, :].rearrange("(k p) x -> p k x", k=KC), zrow[:, :, :]).then_inc(stored, 16)
            sp.wait_ge(built, 1)
            for i in range(2):
                for h in range(2):
                    sp.dma_start(d["taps"][i, h].rearrange("(k p) g -> p k g", k=KC), padded[i][h][:, :, :]).then_inc(stored, 16)
            sp.wait_ge(biased, 1)
            sp.dma_start(d["bias"].rearrange("(k p) -> p k", k=KC), bias[:, :]).then_inc(stored, 16)
            sp.wait_ge(stored, 16 * (2 * IMG + 4 + 1))

        @block.gpsimd
        def _(pool):
            nc.gpsimd.memset(zrow[:, :, :], 0.0).then_inc(zeroed, 1)
            nc.gpsimd.memset(half[:, :, :], -0.5).then_inc(cleared, 1)
            for i in range(2):
                for h in range(2):
                    nc.gpsimd.memset(padded[i][h][:, :, :], 0.0).then_inc(cleared, 1)
            pool.wait_ge(loaded, 16 * nload)
            nc.gpsimd.tensor_scalar(bn[:, 3], bn[:, 3], 1e-5, None, ALU.add).then_inc(var_ok, 1)
            pool.wait_ge(var_ok, 1)
            pool.wait_ge(cleared, 1)
            nc.gpsimd.tensor_tensor(inv[:, :, :], bn[:, 3], half[:, :, :], ALU.pow).then_inc(inv_ok, 1)

        @block.vector
        def _(dve):
            done = [0]

            def then(ins):
                done[0] += 1
                ins.then_inc(chain, 1)
                dve.wait_ge(chain, done[0])

            dve.wait_ge(loaded, 16 * nload)
            dve.wait_ge(inv_ok, 1)
            dve.wait_ge(cleared, 5)
            then(nc.vector.tensor_tensor(inv[:, :, :], inv[:, :, :], bn[:, 0], ALU.mult))
            then(nc.vector.tensor_tensor(shift[:, :, :], inv[:, :, :], bn[:, 2], ALU.mult))
            then(nc.vector.tensor_tensor(shift[:, :, :], bn[:, 1], shift[:, :, :], ALU.subtract))
            nc.vector.reduce_sum(bias[:, :], shift[:, :, :], AX.X).then_inc(biased, 1)
            for k in range(KC):
                then(nc.vector.tensor_scalar(merged[:, k], wt[0][:, k], inv[:, k, 0:1], None, ALU.mult))
                for j in range(1, 7):
                    lo, st = KW // 2 - side[j] // 2 * dilation[j], dilation[j]
                    sub = merged[:, k, lo:KW - lo:st, lo:KW - lo:st]
                    then(nc.vector.scalar_tensor_tensor(sub, wt[j][:, k], inv[:, k, j:j + 1], sub, ALU.mult, ALU.add))
            for i, (src, side_i) in enumerate(((w7, 7), (merged, KW))):
                off = (KW - side_i) // 2
                for h in range(2):
                    for k in range(KC):
                        rows = padded[i][h][:, k, :].rearrange("p (r g) -> p r g", g=GP)[:, GR0 + off:GR0 + off + side_i]
                        then(nc.vector.tensor_copy(rows[:, :, GC0[h] + off:GC0[h] + off + side_i], src[:, k]))
                        if h:
                            n = WRAPC - off
                            then(nc.vector.tensor_copy(rows[:, :, GWRAP + off:GWRAP + off + n], src[:, k, :, 0:n]))
            nc.vector.nop().then_inc(built, 1)


def attention(nc, a, d, X, PS, stack):
    s = Scope(nc, "att", stack)
    XR, XB = 4, 12
    wqk = s.sb("wqk", [CH, KC, 4, 4, 32])
    wv = s.sb("wv", [CH, KC, C])
    wp = s.sb("wp", [CH, KC, C])
    gb = s.sb("gb", [CH, 2, KC])
    pb = s.sb("pb", [128, C])
    ident = s.sb("ident", [128, 128])
    x = s.sb("x", [128, XR, C])
    st = s.sb("st", [128, 2, 6])
    mv = s.sb("mv", [128, 4, 2])
    ve = s.sb("ve", [128, 2])
    rs = s.sb("rs", [128, 4])
    mhalf = s.sb("mhalf", [128, 1])
    xn = s.sb("xn", [128, 2, C])
    xpb = s.sb("xpb", [128, XB, C])
    h = s.sb("h", [CH, 2, KC, 128])
    qk = s.sb("qk", [128, 2, 4, 128])
    vbd = s.sb("vbd", [128, 6, 2, 4, 2, HD + 1])
    mx = s.sb("mx", [128, 2, NH])
    sd = s.sb("sd", [128, 2, 512])
    p = s.sb("p", [128, 4, 512])
    pt = s.sb("pt", [128, 2, 4, 128])
    ri = s.sb("ri", [128, 2, NH])
    o = s.sb("o", [128, 2, C])
    ot = s.sb("ot", [CH, 2, KC, 128])

    psS = PS[:, 0:4, 0:128]
    psPV = PS[:, 0, 128:328]
    psPJ = PS[:, 1, 128:128 + C]
    psT = PS[0:CH, 7, 0:256]
    psOT = PS[0:CH, 7, 256:512]
    psQK = PS[:, 5, :]
    psV = PS[:, 6, 0:C]
    psPT = PS[:, 4, :]

    wloaded, ready, loaded = s.sem("wloaded"), s.sem("ready"), s.sems("loaded", XR)
    names = ("stats", "aggr", "var_ok", "rstd", "xn_ready", "xt", "h_ready", "qk", "qk_ready", "v", "v_ready",
             "scores", "max", "shifted", "probs", "pt", "pt_ready", "pv", "recip", "o_ready", "ot", "ot_ready",
             "proj", "resid", "xpb_ready")
    q = {x: s.sem(x) for x in names}
    READY = 5 + 6 * 2
    HEAD, LAG, U = 16, 9, 12

    with nc.Block() as block:
        @block.sync
        def _(sp):
            nc.sync.dma_start(wv[:, :, :], a["L0_conv_qkv_w"].rearrange("(k p) n -> p k n", k=KC)[:, :, 2 * C:3 * C]).then_inc(wloaded, 16)
            nc.sync.dma_start(wp[:, :, :], a["L0_conv_proj_w"].rearrange("(k p) n -> p k n", k=KC)).then_inc(wloaded, 16)
            nc.sync.dma_start(gb[:, 0, :], a["L0_conv_ln1_g"].rearrange("(k p) -> p k", k=KC)).then_inc(wloaded, 16)
            nc.sync.dma_start(gb[:, 1, :], a["L0_conv_ln1_b"].rearrange("(k p) -> p k", k=KC)).then_inc(wloaded, 16)
            nc.sync.dma_start(pb[:, :], a["L0_conv_proj_b"].partition_broadcast(128)).then_inc(wloaded, 16)
            sp.wait_ge(ready, 1)
            for k in range(KC):
                for ch in range(4):
                    src = a["L0_conv_qkv_w"][k * CH:(k + 1) * CH, ch * CH:(ch + 1) * CH].rearrange("p (h e) -> p h e", e=HD)
                    nc.sync.dma_start(wqk[:, k, ch, :, 0:HD], src).then_inc(wloaded, 16)

            def body(t):
                if t.reached(XR):
                    sp.wait_ge(q["xn_ready"], t.n - XR + 1)
                    sp.wait_ge(q["xpb_ready"], t.n - XR + 1)
                sp.dma_start(x[:, t.buf(XR), :], d["x"][bass.ds(t.n, 1)].rearrange("o p c -> (o p) c")).then_inc(loaded[t.buf(XR)], 16)
            run_steps(sp, NB, U, HEAD, 0, body)

        @block.gpsimd
        def _(pool):
            nc.gpsimd.memset(wqk[:, :, :, :, :], 0.0).then_inc(ready, 1)
            nc.gpsimd.memset(mhalf[:, :], -0.5).then_inc(ready, 1)
            nc.gpsimd.memset(ident[:, :], 0.0).then_inc(ready, 1)
            nc.gpsimd.memset(vbd[:, :, :, :, :, :], 0.0).then_inc(ready, 1)
            pool.wait_ge(ready, 4)
            nc.gpsimd.affine_select(out=ident[:, :], in_=ident[:, :], compare_op=ALU.not_equal, fill=1.0, base=0,
                                    pattern=[[-1, 128]], channel_multiplier=1).then_inc(ready, 1)
            pool.wait_ge(wloaded, 16 * 13)

            def body(t):
                if t.inside(NB):
                    reached = at_hand(pool, t.n + 1)
                    pool.wait_ge(ready, READY)
                    pool.wait_ge(q["aggr"], reached)
                    nc.gpsimd.tensor_scalar(ve[:, t.buf(2):t.buf(2) + 1], mv[:, t.buf(4), 1:2], 1e-5, None, ALU.add).then_inc(q["var_ok"], 1)
                    pool.wait_ge(q["var_ok"], t.n + 1)
                    if t.reached(4):
                        pool.wait_ge(q["xn_ready"], t.n - 3)
                    nc.gpsimd.tensor_tensor(rs[:, t.buf(4):t.buf(4) + 1], ve[:, t.buf(2):t.buf(2) + 1], mhalf[:, :], ALU.pow).then_inc(q["rstd"], 1)
                    if t.reached(XB):
                        pool.wait_ge(q["resid"], t.n - XB + 1)
                    nc.gpsimd.tensor_tensor(xpb[:, t.buf(XB), :], x[:, t.buf(XR), :], pb[:, :], ALU.add).then_inc(q["xpb_ready"], 1)
            run_steps(pool, NB, U, HEAD, 0, body)

        @block.vector
        def _(dve):
            dve.wait_ge(ready, 5)
            for b in range(6):
                for e in range(2):
                    nc.vector.memset(vbd[64 * e:64 * e + 64, b, :, :, e, HD:HD + 1], 1.0).then_inc(ready, 1)

            def body(t):
                b = t.back(4)
                if b.inside(NB):
                    dve.wait_ge(q["scores"], b.n + 1)
                    s4 = psS.rearrange("p h (e m) -> p h e m", e=2)
                    nc.vector.reduce_max(mx[:, b.buf(2), :].rearrange("p (h e) -> p h e", e=2), s4, AX.X).then_inc(q["max"], 1)
                    dve.wait_ge(q["max"], b.n + 1)
                    if b.reached(2):
                        dve.wait_ge(q["probs"], b.n - 1)
                    nc.vector.tensor_tensor(sd[:, b.buf(2), :].rearrange("p (h e m) -> p h e m", h=4, e=2), s4,
                                            view(mx[:, b.buf(2), :], [[2, 4], [1, 2], [0, 64]]), ALU.subtract).then_inc(q["shifted"], 1)
                b = t.back(1)
                if b.inside(NB):
                    dve.wait_ge(q["rstd"], b.n + 1)
                    if b.reached(2):
                        dve.wait_ge(q["xt"], b.n - 1)
                    nc.vector.tensor_scalar(xn[:, b.buf(2), :], x[:, b.buf(XR), :], mv[:, b.buf(4), 0:1], rs[:, b.buf(4):b.buf(4) + 1],
                                            ALU.subtract, ALU.mult).then_inc(q["xn_ready"], 1)
                b = t
                if b.inside(NB):
                    dve.wait_ge(loaded[b.buf(XR)], 16 * (b.turn(XR) + 1))
                    nc.vector.bn_stats(out=st[:, b.buf(2), :], in_=x[:, b.buf(XR), :]).then_inc(q["stats"], 1)
                    reached = at_hand(dve, b.n + 1)
                    dve.wait_ge(ready, READY)
                    dve.wait_ge(q["stats"], reached)
                    nc.vector.bn_aggr(out=mv[:, b.buf(4), :], in_=st[:, b.buf(2), :]).then_inc(q["aggr"], 1)
                b = t.back(9)
                if b.inside(NB):
                    dve.wait_ge(q["proj"], b.n + 1)
                    dve.wait_ge(q["xpb_ready"], b.n + 1)
                    nc.vector.tensor_tensor(at(X, b.n), psPJ, xpb[:, b.buf(XB), :], ALU.add).then_inc(q["resid"], 1)
                b = t.back(7)
                if b.inside(NB):
                    dve.wait_ge(q["pv"], b.n + 1)
                    o4 = psPV.rearrange("p (h e c) -> p h e c", h=4, e=2)
                    nc.vector.reciprocal(ri[:, b.buf(2), :].rearrange("p (h e o) -> p h e o", e=2, o=1), o4[:, :, :, HD:HD + 1]).then_inc(q["recip"], 1)
                    dve.wait_ge(q["recip"], b.n + 1)
                    if b.reached(2):
                        dve.wait_ge(q["ot"], b.n - 1)
                    nc.vector.tensor_tensor(o[:, b.buf(2), :].rearrange("p (e h c) -> p h e c", h=4, e=2), o4[:, :, :, 0:HD],
                                            view(ri[:, b.buf(2), :], [[2, 4], [1, 2], [0, HD]]), ALU.mult).then_inc(q["o_ready"], 1)
                b = t.back(6)
                if b.inside(NB):
                    dve.wait_ge(q["pt"], b.n + 1)
                    if b.reached(2):
                        dve.wait_ge(q["pv"], b.n - 1)
                    nc.vector.tensor_copy(pt[:, b.buf(2), :, :].rearrange("p h n -> p (h n)"), psPT).then_inc(q["pt_ready"], 1)
            run_steps(dve, NB, U, HEAD, LAG, body)

        @block.scalar
        def _(act):
            act.wait_ge(wloaded, 16 * 13)
            act.wait_ge(ready, READY)

            def body(t):
                b = t.back(2)
                if b.inside(NB):
                    act.wait_ge(q["xt"], b.n + 1)
                    if b.reached(2):
                        act.wait_ge(q["v"], b.n - 1)
                    for k in range(KC):
                        last = nc.scalar.activation(h[:, b.buf(2), k, :], psT[:, k * 128:(k + 1) * 128],
                                                    ACT.Identity, bias=gb[:, 1, k:k + 1], scale=gb[:, 0, k:k + 1])
                    last.then_inc(q["h_ready"], 1)
                b = t.back(4)
                if b.inside(NB):
                    act.wait_ge(q["shifted"], b.n + 1)
                    if b.reached(4):
                        act.wait_ge(q["pt"], b.n - 3)
                    nc.scalar.activation(p[:, b.buf(4), :], sd[:, b.buf(2), :], ACT.Exp, scale=float(HD) ** -0.5).then_inc(q["probs"], 1)
                b = t.back(3)
                if b.inside(NB):
                    act.wait_ge(q["qk"], b.n + 1)
                    if b.reached(2):
                        act.wait_ge(q["scores"], b.n - 1)
                    nc.scalar.activation(qk[:, b.buf(2), :, :], psQK.rearrange("p (c n) -> p c n", c=4), ACT.Identity).then_inc(q["qk_ready"], 1)
                    act.wait_ge(q["v"], b.n + 1)
                    if b.reached(6):
                        act.wait_ge(q["pv"], b.n - 5)
                    for w in range(2):
                        for e in range(2):
                            src = psV[64 * w:64 * w + 64, :].rearrange("p (e h c) -> p e h c", e=2, h=4)[:, e]
                            last = nc.scalar.activation(vbd[64 * e:64 * e + 64, b.buf(6), w, :, e, 0:HD], src, ACT.Identity)
                    last.then_inc(q["v_ready"], 1)
                b = t.back(8)
                if b.inside(NB):
                    act.wait_ge(q["ot"], b.n + 1)
                    if b.reached(2):
                        act.wait_ge(q["proj"], b.n - 1)
                    nc.scalar.activation(ot[:, b.buf(2), :, :], psOT.rearrange("p (k n) -> p k n", k=KC), ACT.Identity).then_inc(q["ot_ready"], 1)
            run_steps(act, NB, U, HEAD, LAG, body)

        @block.tensor
        def _(pe):
            pe.wait_ge(wloaded, 16 * 13)
            pe.wait_ge(ready, READY)

            def body(t):
                b = t.back(4)
                if b.inside(NB):
                    pe.wait_ge(q["qk_ready"], b.n + 1)
                    if b.reached(1):
                        pe.wait_ge(q["shifted"], b.n)
                    if b.reached(6):
                        pe.wait_ge(q["resid"], b.n - 5)
                    if b.reached(4):
                        pe.wait_ge(q["o_ready"], b.n - 3)
                    for e in range(2):
                        for w in range(2):
                            for hh in range(4):
                                rows = qk[32 * hh:32 * hh + HD, b.buf(2), :, 64 * w:64 * w + 64]
                                last = nc.tensor.matmul(psS[64 * w:64 * w + 64, hh, 64 * e:64 * e + 64], rows[:, e, :], rows[:, 2 + e, :], start=True, stop=True)
                    last.then_inc(q["scores"], 1)
                b = t.back(2)
                if b.inside(NB):
                    pe.wait_ge(q["xn_ready"], b.n + 1)
                    if b.reached(1):
                        pe.wait_ge(q["h_ready"], b.n)
                    if b.reached(7):
                        pe.wait_ge(q["ot_ready"], b.n - 6)
                    for k in range(KC):
                        last = nc.tensor.transpose(psT[:, k * 128:(k + 1) * 128], xn[:, b.buf(2), k * CH:(k + 1) * CH], ident[:, :])
                    last.then_inc(q["xt"], 1)
                b = t.back(3)
                if b.inside(NB):
                    pe.wait_ge(q["h_ready"], b.n + 1)
                    if b.reached(1):
                        pe.wait_ge(q["qk_ready"], b.n)
                    for ch in range(4):
                        for k in range(KC):
                            last = nc.tensor.matmul(psQK[:, ch * 128:(ch + 1) * 128], wqk[:, k, ch, :, :].rearrange("p h e -> p (h e)"),
                                                    h[:, b.buf(2), k, :], start=(k == 0), stop=(k == KC - 1))
                    last.then_inc(q["qk"], 1)
                b = t.back(9)
                if b.inside(NB):
                    pe.wait_ge(q["ot_ready"], b.n + 1)
                    if b.reached(1):
                        pe.wait_ge(q["resid"], b.n)
                    pe.wait_ge(q["shifted"], b.upto(6))
                    for k in range(KC):
                        last = nc.tensor.matmul(psPJ, ot[:, b.buf(2), k, :], wp[:, k, :], start=(k == 0), stop=(k == KC - 1))
                    last.then_inc(q["proj"], 1)
                b = t.back(7)
                if b.inside(NB):
                    pe.wait_ge(q["pt_ready"], b.n + 1)
                    pe.wait_ge(q["v_ready"], b.n + 1)
                    if b.reached(1):
                        pe.wait_ge(q["o_ready"], b.n)
                    pe.wait_ge(q["shifted"], b.upto(4))
                    for w in range(2):
                        for hp in range(4):
                            last = nc.tensor.matmul(psPV[64 * w:64 * w + 64, hp * 50:hp * 50 + 50], pt[:, b.buf(2), hp, 64 * w:64 * w + 64],
                                                    vbd[:, b.buf(6), w, hp, :, :].rearrange("p e c -> p (e c)"), start=True, stop=True)
                    last.then_inc(q["pv"], 1)
                b = t.back(3)
                if b.inside(NB):
                    if b.reached(1):
                        pe.wait_ge(q["v_ready"], b.n)
                    for k in range(KC):
                        last = nc.tensor.matmul(psV, h[:, b.buf(2), k, :], wv[:, k, :], start=(k == 0), stop=(k == KC - 1))
                    last.then_inc(q["v"], 1)
                b = t.back(8)
                if b.inside(NB):
                    pe.wait_ge(q["o_ready"], b.n + 1)
                    if b.reached(1):
                        pe.wait_ge(q["ot_ready"], b.n)
                    pe.wait_ge(q["h_ready"], b.upto(7))
                    for k in range(KC):
                        last = nc.tensor.transpose(psOT[:, k * 128:(k + 1) * 128], o[:, b.buf(2), k * CH:(k + 1) * CH], ident[:, :])
                    last.then_inc(q["ot"], 1)
                b = t.back(6)
                if b.inside(NB):
                    pe.wait_ge(q["probs"], b.n + 1)
                    if b.reached(1):
                        pe.wait_ge(q["pt_ready"], b.n)
                    for hp in range(4):
                        last = nc.tensor.transpose(psPT[:, hp * 128:hp * 128 + 128], p[:, b.buf(4), hp * 128:hp * 128 + 128], ident[:, :])
                    last.then_inc(q["pt"], 1)
            run_steps(pe, NB, U, HEAD, LAG, body)


class NormUp:

    BANKS = MC // 2

    def __init__(self, nc, s, X, PS, eps, ring):
        self.nc, self.X, self.eps, self.ring = nc, X, eps, ring
        self.w1 = s.parts("w1", [CH, KC, HID])
        self.b1 = s.sb("b1", [128, MC])
        self.gb = s.sb("gb", [CH, 2, KC])
        self.ident = s.sb("ident", [128, 128])
        self.st = s.sb("st", [128, ring, 6])
        self.mv = s.sb("mv", [128, ring, 2])
        self.ve = s.sb("ve", [128, ring])
        self.rs = s.sb("rs", [128, ring])
        self.small = s.sb("small", [128, 2])
        self.xn = s.sb("xn", [128, 2, C])
        self.h = s.parts("h", [CH, 2, KC * 2, 128])
        self.psU = [PS[:, i, :] for i in range(self.BANKS)]
        self.psT = PS[0:CH, 3, :]
        self.psB = PS[:, 4, 0:MC]
        self.q = {x: s.sem(x) for x in ("ready", "loaded", "w1_ready", "shift", "scaled", "high", "stats", "aggr", "var_ok", "rstd",
                                        "xn_ready", "xt", "h_high", "h_ready", "up", "gelu")}

    def load(self, eng, raw, w, b, g, shift):
        for dst, src in ((raw, w.rearrange("(k p) n -> p k n", k=KC)), (self.b1[:, :], b.rearrange("(m p) -> p m", m=MC)),
                         (self.gb[:, 0, :], g.rearrange("(k p) -> p k", k=KC)), (self.gb[:, 1, :], shift.rearrange("(k p) -> p k", k=KC))):
            eng.dma_start(dst, src).then_inc(self.q["loaded"], 16)

    def constants(self, pool):
        self.nc.gpsimd.memset(self.small[:, 0:1], self.eps).then_inc(self.q["ready"], 1)
        self.nc.gpsimd.memset(self.small[:, 1:2], -0.5).then_inc(self.q["ready"], 1)
        self.nc.gpsimd.memset(self.ident[:, :], 0.0).then_inc(self.q["ready"], 1)
        pool.wait_ge(self.q["ready"], 3)
        self.nc.gpsimd.affine_select(out=self.ident[:, :], in_=self.ident[:, :], compare_op=ALU.not_equal, fill=1.0, base=0,
                                     pattern=[[-1, 128]], channel_multiplier=1).then_inc(self.q["ready"], 1)
        pool.wait_ge(self.q["ready"], 4)

    def shift_bias(self, pe, raw):
        pe.wait_ge(self.q["loaded"], 16 * 4)
        for m in range(MC):
            for k in range(KC):
                last = self.nc.tensor.matmul(self.psB[:, m:m + 1], raw[:, k, m * 128:(m + 1) * 128], self.gb[:, 1, k:k + 1],
                                             start=(k == 0), stop=(k == KC - 1))
        last.then_inc(self.q["shift"], 1)
        pe.wait_ge(self.q["ready"], 4)
        pe.wait_ge(self.q["w1_ready"], 2)

    def weights(self, dve, raw):
        nc, q = self.nc, self.q
        dve.wait_ge(q["shift"], 1)
        nc.vector.tensor_tensor(self.b1[:, :], self.b1[:, :], self.psB, ALU.add).then_inc(q["w1_ready"], 1)
        for k in range(KC):
            nc.vector.tensor_scalar(raw[:, k, :], raw[:, k, :], self.gb[:, 0, k:k + 1], None, ALU.mult).then_inc(q["scaled"], 1)
        dve.wait_ge(q["scaled"], KC)
        nc.vector.tensor_copy(self.w1[0][:, :, :], raw).then_inc(q["high"], 1)
        dve.wait_ge(q["high"], 1)
        nc.vector.tensor_tensor(self.w1[1][:, :, :], raw, as_f32(self.w1[0][:, :, :]), ALU.subtract).then_inc(q["w1_ready"], 1)
        dve.wait_ge(q["ready"], 4)

    def stats(self, dve, b):
        nc, q = self.nc, self.q
        nc.vector.bn_stats(out=self.st[:, b.buf(self.ring), :], in_=at(self.X, b.n)).then_inc(q["stats"], 1)
        reached = at_hand(dve, b.n + 1)
        dve.wait_ge(q["ready"], 4)
        dve.wait_ge(q["stats"], reached)
        nc.vector.bn_aggr(out=self.mv[:, b.buf(self.ring), :], in_=self.st[:, b.buf(self.ring), :]).then_inc(q["aggr"], 1)

    def rstd(self, pool, b):
        nc, q = self.nc, self.q
        one = slice(b.buf(self.ring), b.buf(self.ring) + 1)
        pool.wait_ge(q["aggr"], b.n + 1)
        nc.gpsimd.tensor_tensor(self.ve[:, one], self.mv[:, b.buf(self.ring), 1:2], self.small[:, 0:1], ALU.add).then_inc(q["var_ok"], 1)
        pool.wait_ge(q["var_ok"], b.n + 1)
        if b.reached(self.ring):
            pool.wait_ge(q["xn_ready"], b.n - self.ring + 1)
        nc.gpsimd.tensor_tensor(self.rs[:, one], self.ve[:, one], self.small[:, 1:2], ALU.pow).then_inc(q["rstd"], 1)

    def normalize(self, dve, pair):
        nc, q = self.nc, self.q
        if pair.reached(1):
            dve.wait_ge(q["xt"], pair.n)
        for b in pair.blocks():
            dve.wait_ge(q["rstd"], b.n + 1)
            one = b.buf(self.ring)
            nc.vector.tensor_scalar(self.xn[:, b.buf(2), :], at(self.X, b.n), self.mv[:, one, 0:1], self.rs[:, one:one + 1],
                                    ALU.subtract, ALU.mult).then_inc(q["xn_ready"], 1)

    def transpose(self, pe, pair):
        nc, q = self.nc, self.q
        pe.wait_ge(q["xn_ready"], pair.n * 2 + 2)
        if pair.reached(1):
            pe.wait_ge(q["h_ready"], pair.n)
        for k in range(KC):
            for i in range(2):
                at_ = (2 * k + i) * 128
                last = nc.tensor.transpose(self.psT[:, at_:at_ + 128], self.xn[:, i, k * CH:(k + 1) * CH], self.ident[:, :])
        last.then_inc(q["xt"], 1)

    def pieces(self, part, pair, swapped):
        h = part[:, pair.buf(2)]
        if not swapped:
            return [(h.rearrange("p g n -> p (g n)"), self.psT)]
        ordered = h.rearrange("p group (half line col) -> p group half line col", half=2, line=8)
        tokens = self.psT.rearrange("p (group line half col) -> p group line half col", group=2 * KC, line=8, half=2)
        return [(ordered[:, :, i], tokens[:, :, :, i]) for i in range(2)]

    def high(self, act, pair, swapped=False):
        nc, q = self.nc, self.q
        act.wait_ge(q["xt"], pair.n + 1)
        if pair.reached(2):
            act.wait_ge(q["up"], (pair.n - 1) * self.BANKS)
        for dst, src in self.pieces(self.h[0], pair, swapped):
            last = nc.scalar.activation(dst, src, ACT.Identity)
        last.then_inc(q["h_high"], 1)

    def low(self, dve, pair, swapped=False):
        nc, q = self.nc, self.q
        dve.wait_ge(q["h_high"], pair.n + 1)
        for (dst, src), (high, _) in zip(self.pieces(self.h[1], pair, swapped), self.pieces(as_f32(self.h[0][:, :, :, :]), pair, swapped)):
            last = nc.vector.tensor_tensor(dst, src, high, ALU.subtract)
        last.then_inc(q["h_ready"], 1)

    def up(self, pe, pair):
        nc, q = self.nc, self.q
        pe.wait_ge(q["h_ready"], pair.n + 1)
        for i in range(self.BANKS):
            if pair.reached(1):
                pe.wait_ge(q["gelu"], (pair.n - 1) * self.BANKS + i + 1)
            for e in range(2):
                m = slice((2 * i + e) * 128, (2 * i + e + 1) * 128)
                last = product(nc, self.psU[i][:, e * 256:(e + 1) * 256], lambda k: [w[:, k, m] for w in self.w1],
                               lambda k: [h[:, pair.buf(2), 2 * k:2 * k + 2, :].rearrange("p g n -> p (g n)") for h in self.h], KC)
            last.then_inc(q["up"], 1)

    def gelu(self, act, pair, hid):
        nc, q = self.nc, self.q
        for i in range(self.BANKS):
            act.wait_ge(q["up"], pair.n * self.BANKS + i + 1)
            for e in range(2):
                m = 2 * i + e
                last = nc.scalar.activation(hid[:, m, :], self.psU[i][:, e * 256:(e + 1) * 256], ACT.Gelu, bias=self.b1[:, m:m + 1])
            last.then_inc(q["gelu"], 1)


def mlp(nc, a, d, X, PS, stack):
    s = Scope(nc, "mlp", stack)
    n = NormUp(nc, s, X, PS, 1e-5, BX)
    w2 = s.sb("w2", [128, MC, C])
    b2 = s.sb("b2", [128, C])
    x1 = s.sb("x1", [128, 2, C])
    strips = s.sb("strips", [128, 2 * KC * ROW])
    strip = strips[0:CH, :].rearrange("p (t k r x) -> p t k r x", t=2, k=KC, r=8)
    w1raw = strips[0:CH, 0:KC * HID].rearrange("p (k n) -> p k n", k=KC)
    hid = s.sb("hid", [128, 2, MC, 256])
    psT1 = PS[0:CH, 5, :]
    psD = [PS[:, 6 + i, 0:C] for i in range(2)]
    q = {x: s.sem(x) for x in ("w2loaded", "biased", "down", "x1_ready", "kept", "x1t", "strip_ready")}
    stored = s.sems("stored", 2)
    U, HEAD, LAG = 14, 14, 5

    with nc.Block() as block:
        @block.sync
        def _(sp):
            n.load(sp, w1raw, a["L0_conv_fc1_w"], a["L0_conv_fc1_b"], a["L0_conv_ln2_g"], a["L0_conv_ln2_b"])
            sp.dma_start(w2[:, :, :], a["L0_conv_fc2_w"].rearrange("(m p) n -> p m n", m=MC)).then_inc(q["w2loaded"], 16)
            sp.dma_start(b2[:, :], a["L0_conv_fc2_b"].partition_broadcast(128)).then_inc(q["w2loaded"], 16)
            for img in range(IMG):
                with sp.Fori(0, BY // 2) as g:
                    for j in range(2):
                        t = g * 2 + (j + img * BY)
                        sp.wait_ge(q["strip_ready"], t * BX + BX)
                        sp.dma_start(d["x1"][img, :, bass.ds(g * 16 + (8 * j + 1), 8), :].rearrange("(k p) r x -> p k (r x)", k=KC),
                                     strip[:, j, :, :, :].rearrange("p k r x -> p k (r x)")).then_inc(stored[j], 16)
            for j in range(2):
                sp.wait_ge(stored[j], 16 * (NS // 2))

        @block.gpsimd
        def _(pool):
            n.constants(pool)
            pool.wait_ge(q["w2loaded"], 32)

            def body(t):
                p = t.back(5)
                if p.inside(NP):
                    for b in p.blocks():
                        reached = at_hand(pool, b.n + 1)
                        pool.wait_ge(q["w2loaded"], 32)
                        pool.wait_ge(q["x1_ready"], reached)
                        nc.gpsimd.tensor_copy(at(X, b.n), x1[:, b.buf(2), :]).then_inc(q["kept"], 1)
                p = t.back(1)
                if p.inside(NP):
                    for b in p.blocks():
                        pool.wait_ge(n.q["xn_ready"], b.n + 1)
                        nc.gpsimd.tensor_tensor(at(X, b.n), at(X, b.n), b2[:, :], ALU.add).then_inc(q["biased"], 1)
                if t.inside(NP):
                    for b in t.blocks():
                        n.rstd(pool, b)
            run_steps(pool, NP, U, HEAD, LAG, body)

        @block.vector
        def _(dve):
            n.weights(dve, w1raw)

            def body(t):
                p = t.back(1)
                if p.inside(NP):
                    n.normalize(dve, p)
                if t.inside(NP):
                    for b in t.blocks():
                        n.stats(dve, b)
                p = t.back(2)
                if p.inside(NP):
                    n.low(dve, p)
                p = t.back(4)
                if p.inside(NP):
                    if p.reached(1):
                        dve.wait_ge(q["x1t"], p.n)
                        dve.wait_ge(q["kept"], p.n * 2)
                    for b in p.blocks():
                        dve.wait_ge(q["down"], b.n + 1)
                        dve.wait_ge(q["biased"], b.n + 1)
                        nc.vector.tensor_tensor(x1[:, b.buf(2), :], psD[b.buf(2)], at(X, b.n), ALU.add).then_inc(q["x1_ready"], 1)
            run_steps(dve, NP, U, HEAD, LAG, body)

        @block.scalar
        def _(act):
            act.wait_ge(n.q["w1_ready"], 2)

            def body(t):
                p = t.back(2)
                if p.inside(NP):
                    n.high(act, p)
                p = t.back(5)
                if p.inside(NP):
                    act.wait_ge(q["x1t"], p.n + 1)
                    for i, b in enumerate(p.blocks()):
                        if b.reached(2 * BX) and b.buf(BX) == 0:
                            act.wait_ge(stored[b.buf(2 * BX) // BX], b.turn(2 * BX) * 16)
                        for k in range(KC):
                            dst = strip[:, b.buf(2 * BX) // BX, k, :, b.buf(BX) * 16:b.buf(BX) * 16 + 16].rearrange("p r (w c) -> p w r c", w=2)
                            src = psT1[:, (2 * i + k) * 128:(2 * i + k + 1) * 128].rearrange("p (w r c) -> p w r c", w=2, r=8)
                            last = nc.scalar.activation(dst, src, ACT.Identity)
                        last.then_inc(q["strip_ready"], 1)
                p = t.back(3)
                if p.inside(NP):
                    if p.reached(2):
                        act.wait_ge(q["down"], p.n * 2 - 2)
                    n.gelu(act, p, hid[:, p.buf(2)])
            run_steps(act, NP, U, HEAD, LAG, body)

        @block.tensor
        def _(pe):
            n.shift_bias(pe, w1raw)
            pe.wait_ge(q["w2loaded"], 32)

            def down(p, i):
                b = p.blocks()[i]
                pe.wait_ge(n.q["gelu"], p.n * n.BANKS + n.BANKS)
                if b.reached(2):
                    pe.wait_ge(q["x1_ready"], b.n - 1)
                for m in range(MC):
                    last = nc.tensor.matmul(psD[i], hid[:, p.buf(2), m, i * 128:(i + 1) * 128], w2[:, m, :], start=(m == 0), stop=(m == MC - 1))
                last.then_inc(q["down"], 1)

            def body(t):
                p = t.back(2)
                if p.inside(NP):
                    n.transpose(pe, p)
                p = t.back(4)
                if p.inside(NP):
                    down(p, 0)
                p = t.back(5)
                if p.inside(NP):
                    pe.wait_ge(q["x1_ready"], p.n * 2 + 2)
                    if p.reached(1):
                        pe.wait_ge(q["strip_ready"], p.n * 2)
                    for i in range(2):
                        for k in range(KC):
                            last = nc.tensor.transpose(psT1[:, (2 * i + k) * 128:(2 * i + k + 1) * 128], x1[:, i, k * CH:(k + 1) * CH], n.ident[:, :])
                    last.then_inc(q["x1t"], 1)
                p = t.back(3)
                if p.inside(NP):
                    n.up(pe, p)
                p = t.back(4)
                if p.inside(NP):
                    down(p, 1)
            run_steps(pe, NP, U, HEAD, LAG, body)


def sobel(nc, a, d, X, PS, stack):
    s = Scope(nc, "sobel", stack)
    wf = s.sb("wf", [CH + 1, 2 * KC, C])
    row = s.sb("row", [128, 2, C])
    xin = s.sb("xin", [CH, KC, 10, HW + 2])
    down = s.sb("down", [CH, 8, HW + 2])
    diff = s.sb("diff", [CH, 8, HW + 2])
    half = s.sb("half", [CH, 8, HW + 1])
    edge = s.sb("edge", [CH + 1, 2, 2 * KC, BX, 128])
    f = s.sb("f", [128, BX, C])
    st = s.sb("st", [128, BX, 6])
    mv = s.sb("mv", [128, BX, 2])
    ve = s.sb("ve", [128, BX])
    rs = s.sb("rs", [128, BX])
    nb = s.sb("nb", [128, BX])
    small = s.sb("small", [128, 2, BX])
    loaded = s.sems("loaded", KC)
    q = {x: s.sem(x) for x in ("wloaded", "ready", "down1", "down2", "ex", "diff", "half", "ey", "fused", "stats", "aggr", "var_ok",
                               "rstd", "shift", "normed", "scaled", "affine", "gelu", "added", "stored")}
    U, HEAD, LAG = 2, 4, 3
    SLAG = 4
    READY = 4

    def psF(t, j):
        return PS[:, 4 * t.buf(2) + j // 2, j % 2 * 256:j % 2 * 256 + C]

    def in_blocks(t, e):
        return view(edge[0:CH, t.buf(2), e, 0, 0:1], [[8, 8], [64, 2 * BX], [1, 8]])

    def per_block(i):
        return view(row[:, i, 0:1], [[0, BX], [1, C]])

    def rows8(ap):
        return ap.rearrange("p r (b c) -> p r b c", c=8)

    with nc.Block() as block:
        @block.sync
        def _(sp):
            sp.dma_start(wf[0:CH, :, :], a["L1_conv_fusion_wT"].rearrange("(k p) n -> p k n", p=CH)).then_inc(q["wloaded"], 16)
            sp.dma_start(wf[CH:CH + 1, 0, :], a["L1_conv_fusion_b"].partition_broadcast(1)).then_inc(q["wloaded"], 16)
            for i, name in enumerate(("ln_w", "ln_b")):
                sp.dma_start(row[:, i, :], a["L1_conv_" + name].partition_broadcast(128)).then_inc(q["wloaded"], 16)
            sp.wait_ge(q["ready"], READY)

            def load(t, img, r):
                for k in range(KC):
                    if t.reached(1):
                        sp.wait_ge(q["down2"], t.n * KC + k - KC + 1)
                        sp.wait_ge(q["diff"], t.n * KC + k - KC + 1)
                    sp.dma_start(xin[:, k, :, 1:HW + 1], d["x1"][img, k * CH:(k + 1) * CH, r, :]).then_inc(loaded[k], 16)

            def store(t):
                sp.wait_ge(q["added"], t.n + 1)
                sp.dma_start(d["x2"][bass.ds(t.n * BX, BX)].rearrange("b p c -> p b c"), X[:, bass.ds(t.n * BX, BX), :]).then_inc(q["stored"], 16)

            for img in range(IMG):
                for j in range(SLAG):
                    t = Step(0, img * BY + j, 1)
                    load(t, img, slice(8 * j, 8 * j + 10))
                    if t.reached(SLAG):
                        store(t.back(SLAG))
                with sp.Fori(SLAG, BY) as g:
                    load(Step(g, img * BY, 1), img, bass.ds(g * 8, 10))
                    store(Step(g, img * BY - SLAG, 1))
            for j in range(NS - SLAG, NS):
                store(Step(0, j, 1))
            sp.wait_ge(q["stored"], 16 * NS)

        @block.gpsimd
        def _(pool):
            for i, (where, what) in enumerate(((xin[:, :, :, 0:HW + 2:HW + 1], 0.0), (edge[CH:CH + 1, :, 0, :, :], 1.0),
                                               (small[:, 0, :], 1e-5), (small[:, 1, :], -0.5))):
                nc.gpsimd.memset(where, what).then_inc(q["ready"], 1)
                pool.wait_ge(q["ready"], i + 1)

            def edge_y(t, k):
                b = t.n * KC + k
                pool.wait_ge(loaded[k], t.n * 16 + 16)
                if t.reached(1) or k:
                    pool.wait_ge(q["half"], b)
                nc.gpsimd.tensor_tensor(diff[:, :, :], xin[:, k, 2:10, :], xin[:, k, 0:8, :], ALU.subtract).then_inc(q["diff"], 1)
                pool.wait_ge(q["diff"], b + 1)
                if t.reached(1) or k:
                    pool.wait_ge(q["ey"], b)
                nc.gpsimd.tensor_tensor(half[:, :, :], diff[:, :, 1:HW + 2], diff[:, :, 0:HW + 1], ALU.add).then_inc(q["half"], 1)
                pool.wait_ge(q["half"], b + 1)
                if t.reached(2):
                    pool.wait_ge(q["fused"], t.n * BX - BX)
                nc.gpsimd.tensor_tensor(in_blocks(t, KC + k), rows8(half[:, :, 1:HW + 1]), rows8(half[:, :, 0:HW]), ALU.add).then_inc(q["ey"], 1)

            def body(t):
                if t.inside(NS):
                    edge_y(t, 0)
                b = t.back(2)
                if b.inside(NS):
                    pool.wait_ge(q["aggr"], b.n * BX + BX)
                    if b.reached(1):
                        pool.wait_ge(q["rstd"], b.n)
                    nc.gpsimd.tensor_tensor(ve[:, :], mv[:, :, 1], small[:, 0, :], ALU.add).then_inc(q["var_ok"], 1)
                    pool.wait_ge(q["var_ok"], b.n + 1)
                    if b.reached(1):
                        pool.wait_ge(q["normed"], b.n * BX)
                    nc.gpsimd.tensor_tensor(rs[:, :], ve[:, :], small[:, 1, :], ALU.pow).then_inc(q["rstd"], 1)
                    pool.wait_ge(q["rstd"], b.n + 1)
                if t.inside(NS):
                    edge_y(t, 1)
            run_steps(pool, NS, U, HEAD, LAG, body)

        @block.vector
        def _(dve):
            dve.wait_ge(q["ready"], READY)
            dve.wait_ge(q["wloaded"], 64)

            def edge_x(t, k):
                b = t.n * KC + k
                dve.wait_ge(loaded[k], t.n * 16 + 16)
                if t.reached(1) or k:
                    dve.wait_ge(q["ex"], b)
                nc.vector.scalar_tensor_tensor(down[:, :, :], xin[:, k, 1:9, :], 2.0, xin[:, k, 0:8, :], ALU.mult, ALU.add).then_inc(q["down1"], 1)
                dve.wait_ge(q["down1"], b + 1)
                nc.vector.tensor_tensor(down[:, :, :], down[:, :, :], xin[:, k, 2:10, :], ALU.add).then_inc(q["down2"], 1)
                dve.wait_ge(q["down2"], b + 1)
                if t.reached(2):
                    dve.wait_ge(q["fused"], t.n * BX - BX)
                nc.vector.tensor_tensor(in_blocks(t, k), rows8(down[:, :, 2:HW + 2]), rows8(down[:, :, 0:HW]), ALU.subtract).then_inc(q["ex"], 1)

            def body(t):
                b = t.back(2)
                if b.inside(NS):
                    if b.reached(1):
                        dve.wait_ge(q["aggr"], b.n * BX)
                    for j in range(BX):
                        if j % 2 == 0:
                            dve.wait_ge(q["fused"], b.n * BX + min(j + 2, BX))
                        nc.vector.bn_stats(out=st[:, j, :], in_=psF(b, j)).then_inc(q["stats"], 1)
                    if b.reached(1):
                        dve.wait_ge(q["shift"], b.n)
                        dve.wait_ge(q["var_ok"], b.n)
                    for j in range(BX):
                        reached = at_hand(dve, b.n * BX + j + 1)
                        dve.wait_ge(q["ready"], READY)
                        dve.wait_ge(q["stats"], reached)
                        nc.vector.bn_aggr(out=mv[:, j, :], in_=st[:, j, :]).then_inc(q["aggr"], 1)
                done = t.back(3)
                if done.inside(NS):
                    dve.wait_ge(q["gelu"], done.n + 1)
                    strip = X[:, bass.ds(done.n * BX, BX), :]
                    nc.vector.tensor_tensor(strip, strip, f[:, :, :], ALU.add).then_inc(q["added"], 1)
                if t.inside(NS):
                    edge_x(t, 0)
                if b.inside(NS):
                    dve.wait_ge(q["rstd"], b.n + 1)
                    dve.wait_ge(q["aggr"], b.n * BX + BX)
                    if b.reached(1):
                        dve.wait_ge(q["normed"], b.n * BX)
                    nc.vector.scalar_tensor_tensor(nb[:, :], mv[:, :, 0], -1.0, rs[:, :], ALU.mult, ALU.mult).then_inc(q["shift"], 1)
                if t.inside(NS):
                    edge_x(t, 1)
                if b.inside(NS):
                    dve.wait_ge(q["normed"], b.n * BX + BX)
                    nc.vector.tensor_tensor(f[:, :, :], f[:, :, :], per_block(0), ALU.mult).then_inc(q["scaled"], 1)
                    dve.wait_ge(q["scaled"], b.n + 1)
                    nc.vector.tensor_tensor(f[:, :, :], f[:, :, :], per_block(1), ALU.add).then_inc(q["affine"], 1)
            run_steps(dve, NS, U, HEAD, LAG, body)

        @block.scalar
        def _(act):
            def body(t):
                b = t.back(2)
                if b.inside(NS):
                    act.wait_ge(q["shift"], b.n + 1)
                    act.wait_ge(q["rstd"], b.n + 1)
                    if b.reached(1):
                        act.wait_ge(q["added"], b.n)
                    for j in range(BX):
                        nc.scalar.activation(f[:, j, :], psF(b, j), ACT.Identity, bias=nb[:, j:j + 1], scale=rs[:, j:j + 1]).then_inc(q["normed"], 1)
                    act.wait_ge(q["affine"], b.n + 1)
                    nc.scalar.activation(f[:, :, :], f[:, :, :], ACT.Gelu).then_inc(q["gelu"], 1)
            run_steps(act, NS, U, HEAD, 2, body)

        @block.tensor
        def _(pe):
            pe.wait_ge(q["wloaded"], 64)
            pe.wait_ge(q["ready"], READY)

            def body(t):
                pe.wait_ge(q["ex"], t.n * KC + KC)
                pe.wait_ge(q["ey"], t.n * KC + KC)
                if t.reached(2):
                    pe.wait_ge(q["normed"], t.n * BX - BX)
                for j in range(BX):
                    for e in range(2 * KC):
                        rows = CH + 1 if e == 0 else CH
                        last = nc.tensor.matmul(psF(t, j), edge[0:rows, t.buf(2), e, j, :], wf[0:rows, e, :], start=(e == 0), stop=(e == 2 * KC - 1))
                    last.then_inc(q["fused"], 1)
            run_steps(pe, NS, U, HEAD, 0, body)


def depthwise(nc, tag, turn, q, loaded, taps, bias, X, PS, out, stack):
    s = Scope(nc, tag, stack)
    U, HEAD, LAG, R = 4, 8, 2, 2
    raw = s.sb("raw", [128, U, GRUN])
    mats = s.sb("mats", [128, R, 2, 24, 16])
    xc = s.sb("xc", [128, R, IMG, BY, BX])
    xs = s.sb("xs", [128, R, IMG * BY, BX])
    brow = s.sb("brow", [128, C])
    res = s.sb("res", [128, 2, U, NB]) if out is not None else None
    first = turn * C
    stored = s.sems("stored", 2) if out is not None else None

    def ps(b):
        return PS[:, b.buf(4), 0:NB].rearrange("p (i y x) -> p i y x", i=IMG, y=BY)

    def toeplitz(b, shifted):
        return view(raw[:, b.buf(U), 0:1], [[-GP, 24], [-1, 16]], 23 * GP + 15 + 16 * shifted)

    with nc.Block() as block:
        @block.sync
        def _(sp):
            sp.dma_start(brow[:, :], bias.partition_broadcast(128)).then_inc(q["bloaded"], 16)

            def body(t):
                b = t.ahead(first)
                if b.reached(U):
                    sp.wait_ge(q["mats_a"], b.n - U + 1)
                    sp.wait_ge(q["mats_b"], b.n - U + 1)
                for h in range(2):
                    src = bass.AP(taps.tensor, taps.offset + h * C * GSZ + t.n * GSZ, [[GP, 8], [1, 8], [1, GRUN]])
                    sp.dma_start(raw[64 * h:64 * h + 64, b.buf(U), :], src).then_inc(loaded[b.buf(U)], 16)
            run_steps(sp, C, U, HEAD, 0, body)

        @block.gpsimd
        def _(pool):
            nc.gpsimd.memset(xs[:, :, :, :], 0.0).then_inc(q["ready"], 1)
            pool.wait_ge(q["ready"], turn + 1)

            def body(t):
                b = t.ahead(first)
                reached = at_hand(pool, b.n - R + 1)
                pool.wait_ge(q["ready"], turn + 1)
                if b.reached(R):
                    pool.wait_ge(q["conv"], reached)
                for h in range(2):
                    if h:
                        pool.wait_ge(q["xs_half"], b.n + 1)
                    src = X[64 * h:64 * h + 64, :, bass.ds(t.n, 1)].rearrange("p (y x) o -> p y (x o)", x=BX)
                    dst = xs[64 * h:64 * h + 64, b.buf(R), :, :]
                    last = nc.gpsimd.tensor_copy(dst[:, :, h:h + BX - 1], src[:, :, 1 - h:BX - h])
                    if not h:
                        last.then_inc(q["xs_half"], 1)
                last.then_inc(q["xs_ready"], 1)
            run_steps(pool, C, U, HEAD, 0, body)

        @block.vector
        def _(dve):
            def body(t):
                b = t.ahead(first)
                if b.reached(R):
                    dve.wait_ge(q["conv"], b.n - R + 1)
                nc.vector.tensor_copy(xc[:, b.buf(R)].rearrange("p i y x -> p (i y x)"), X[:, :, bass.ds(t.n, 1)].rearrange("p b o -> p (b o)"))\
                    .then_inc(q["xc_ready"], 1)
                dve.wait_ge(loaded[b.buf(U)], b.turn(U) * 32 + 32)
                nc.vector.tensor_copy(mats[:, b.buf(R), 0], toeplitz(b, 0)).then_inc(q["mats_a"], 1)
            run_steps(dve, C, U, HEAD, 0, body)

        @block.scalar
        def _(act):
            act.wait_ge(q["bloaded"], 16 * (turn + 1))

            def body(t):
                if t.inside(C):
                    b = t.ahead(first)
                    if b.reached(R):
                        act.wait_ge(q["conv"], b.n - R + 1)
                    act.wait_ge(loaded[b.buf(U)], b.turn(U) * 32 + 32)
                    nc.scalar.activation(mats[:, b.buf(R), 1], toeplitz(b, 1), ACT.Identity).then_inc(q["mats_b"], 1)
                c = t.back(2)
                if c.inside(C):
                    b = c.ahead(first)
                    act.wait_ge(q["conv"], b.n + 1)
                    src = PS[:, b.buf(4), 0:NB]
                    if out is None:
                        dst = X[:, :, bass.ds(c.n, 1)].rearrange("p b o -> p (b o)")
                    else:
                        dst = res[:, c.buf(2 * U) // U, c.buf(U), :]
                        if c.reached(2 * U) and c.buf(U) == 0:
                            act.wait_ge(stored[c.buf(2 * U) // U], c.turn(2 * U) * 16)
                    nc.scalar.activation(dst, src, ACT.Identity, bias=brow[:, bass.ds(c.n, 1)]).then_inc(q["result"], 1)
                    if out is not None and c.buf(U) == U - 1:
                        act.wait_ge(q["result"], b.n + 1)
                        act.dma_start(out[bass.ds(c.n - (U - 1), U)].rearrange("c p b -> p c b"), res[:, c.buf(2 * U) // U]).then_inc(stored[c.buf(2 * U) // U], 16)
            run_steps(act, C, 2 * U, HEAD, LAG, body)
            if out is not None:
                for j in range(2):
                    act.wait_ge(stored[j], 16 * (C // U // 2))

        @block.tensor
        def _(pe):
            def body(t):
                b = t.ahead(first)
                pe.wait_ge(q["xc_ready"], b.n + 1)
                pe.wait_ge(q["xs_ready"], b.n + 1)
                pe.wait_ge(q["mats_a"], b.n + 1)
                pe.wait_ge(q["mats_b"], b.n + 1)
                if b.reached(4):
                    pe.wait_ge(q["result"], b.n - 3)
                src = (xc[:, b.buf(R)], xs[:, b.buf(R)].rearrange("p (i y) x -> p i y x", i=IMG))
                for i, (oy, sh) in enumerate(((0, 0), (0, 1), (-1, 0), (-1, 1), (1, 0), (1, 1))):
                    ylo, yhi = max(0, -oy), BY - max(0, oy)
                    m = mats[:, b.buf(R), sh, 8 * (1 - oy):8 * (1 - oy) + 8, :].rearrange("p r c -> p (r c)")
                    last = nc.tensor.matmul(ps(b)[:, :, ylo:yhi, :], m, src[sh][:, :, ylo + oy:yhi + oy, :], start=(i == 0), stop=(i == 5))
                last.then_inc(q["conv"], 1)
            run_steps(pe, C, U, HEAD, 0, body)


def hidden(nc, a, d, X, PS, ss, stack):
    s = Scope(nc, "hid", stack)
    HR = 3
    n = NormUp(nc, s, X, PS, 1e-6, 4)
    hid = s.sb("hid", [128, HR, MC, 256])
    w1raw = hid[0:CH, 0, :, :].rearrange("p m n -> p (m n)").rearrange("p (k n) -> p k n", k=KC)
    sq = s.sb("sq", [128, 2, MC // 2, 256])
    q = {x: s.sem(x) for x in ("sq", "sq_act", "ss")}
    stored = s.sems("stored", HR)
    U, HEAD, LAG = 6, 8, 4
    BY_ACT = 2

    with nc.Block() as block:
        @block.sync
        def _(sp):
            n.load(sp, w1raw, a["L2_conv_w1"], a["L2_conv_b1"], a["L2_conv_ln_w"], a["L2_conv_ln_b"])

            def body(p):
                sp.wait_ge(n.q["gelu"], p.n * n.BANKS + n.BANKS)
                for i, b in enumerate(p.blocks()):
                    sp.dma_start(d["hid"][bass.ds(b.n, 1)].rearrange("o p m t -> (o p) m t"), hid[:, p.buf(HR), :, i * 128:(i + 1) * 128])\
                        .then_inc(stored[p.buf(HR)], 16)
            run_steps(sp, NP, U, HEAD, 0, body)
            for j in range(HR):
                sp.wait_ge(stored[j], 32 * len(range(j, NP, HR)))

        @block.gpsimd
        def _(pool):
            n.constants(pool)

            def body(t):
                p = t.back(4)
                if p.inside(NP):
                    for e in range(2):
                        pool.wait_ge(n.q["gelu"], p.n * n.BANKS + n.BANKS)
                        if p.reached(1):
                            pool.wait_ge(q["ss"], p.n * 2 + e - 1)
                        own = MC // 2 - (BY_ACT if e else 0)
                        hb = hid[:, p.buf(HR), e * MC // 2:e * MC // 2 + own, :]
                        nc.gpsimd.tensor_tensor(sq[:, e, 0:own], hb, hb, ALU.mult).then_inc(q["sq"], 1)
                if t.inside(NP):
                    for b in t.blocks():
                        n.rstd(pool, b)
            run_steps(pool, NP, U, HEAD, LAG, body)

        @block.vector
        def _(dve):
            n.weights(dve, w1raw)

            def body(t):
                p = t.back(1)
                if p.inside(NP):
                    n.normalize(dve, p)
                if t.inside(NP):
                    for b in t.blocks():
                        n.stats(dve, b)
                p = t.back(2)
                if p.inside(NP):
                    n.low(dve, p, swapped=True)
                p = t.back(4)
                if p.inside(NP):
                    for e in range(2):
                        dve.wait_ge(q["sq"], p.n * 2 + e + 1)
                        if e:
                            dve.wait_ge(q["sq_act"], p.n + 1)
                        nc.vector.reduce_sum(at(ss, p.n)[:, e * MC // 2:(e + 1) * MC // 2], sq[:, e], AX.X).then_inc(q["ss"], 1)
            run_steps(dve, NP, U, HEAD, LAG, body)

        @block.scalar
        def _(act):
            act.wait_ge(n.q["w1_ready"], 2)

            def body(t):
                p = t.back(2)
                if p.inside(NP):
                    n.high(act, p, swapped=True)
                p = t.back(4)
                if p.inside(NP):
                    act.wait_ge(n.q["gelu"], p.n * n.BANKS + n.BANKS)
                    if p.reached(1):
                        act.wait_ge(q["ss"], p.n * 2)
                    nc.scalar.activation(sq[:, 1, MC // 2 - BY_ACT:], hid[:, p.buf(HR), MC - BY_ACT:, :], ACT.Square).then_inc(q["sq_act"], 1)
                p = t.back(3)
                if p.inside(NP):
                    if p.reached(HR):
                        act.wait_ge(stored[p.buf(HR)], p.turn(HR) * 32)
                        act.wait_ge(q["sq"], (p.n - HR) * 2 + 2)
                        act.wait_ge(q["sq_act"], p.n - HR + 1)
                    n.gelu(act, p, hid[:, p.buf(HR)])
            run_steps(act, NP, U, HEAD, LAG, body)

        @block.tensor
        def _(pe):
            n.shift_bias(pe, w1raw)

            def body(t):
                p = t.back(2)
                if p.inside(NP):
                    n.transpose(pe, p)
                p = t.back(3)
                if p.inside(NP):
                    n.up(pe, p)
            run_steps(pe, NP, U, HEAD, LAG, body)


def response_norm(nc, a, PS, ss, gain2, cvec, stack):
    s = Scope(nc, "grn", stack)
    w2 = s.sb("w2", [128, MC, C])
    gbv = s.sb("gbv", [128, 2, MC])
    beta = s.sb("beta", [128, MC, 128])
    b2 = s.sb("b2", [128, C])
    ones = s.sb("ones", [128, 128])
    phalf = s.sb("phalf", [128, IMG, MC])
    tot = s.sb("tot", [128, IMG, MC])
    gx = s.sb("gx", [128, IMG, MC])
    mean = s.sb("mean", [128, IMG])
    scale = s.sb("scale", [128, IMG, MC])
    psM = PS[:, 0, 0:IMG * MC]
    psC = PS[:, 1, 0:C]
    g = {x: s.sem(x) for x in ("loaded", "ready", "tot", "gx", "sums", "chain", "beta", "const")}
    with nc.Block() as block:
        @block.sync
        def _(sp):
            sp.dma_start(w2[:, :, :], a["L2_conv_w2"].rearrange("(m p) n -> p m n", m=MC)).then_inc(g["loaded"], 16)
            sp.dma_start(gbv[:, 0, :], a["L2_conv_grn_gamma"].rearrange("(m p) -> p m", m=MC)).then_inc(g["loaded"], 16)
            sp.dma_start(gbv[:, 1, :], a["L2_conv_grn_beta"].rearrange("(m p) -> p m", m=MC)).then_inc(g["loaded"], 16)
            sp.dma_start(b2[:, :], a["L2_conv_b2"].partition_broadcast(128)).then_inc(g["loaded"], 16)

        @block.gpsimd
        def _(pool):
            nc.gpsimd.memset(ones[:, :], 1.0).then_inc(g["ready"], 1)
            nc.gpsimd.memset(phalf[:, :, :], 0.5).then_inc(g["ready"], 1)
            pool.wait_ge(g["ready"], 2)
            pool.wait_ge(g["tot"], 1)
            nc.gpsimd.tensor_tensor(gx[:, :, :], tot[:, :, :], phalf[:, :, :], ALU.pow).then_inc(g["gx"], 1)

        @block.tensor
        def _(pe):
            pe.wait_ge(g["gx"], 1)
            nc.tensor.matmul(psM, ones[:, :], gx[:, :, :].rearrange("p i m -> p (i m)"), start=True, stop=True).then_inc(g["sums"], 1)
            pe.wait_ge(g["loaded"], 64)
            pe.wait_ge(g["beta"], 1)
            for m in range(MC):
                last = nc.tensor.matmul(psC, beta[:, m, :], w2[:, m, :], start=(m == 0), stop=(m == MC - 1))
            last.then_inc(g["const"], 1)

        @block.vector
        def _(dve):
            done = [0]

            def then(ins):
                done[0] += 1
                ins.then_inc(g["chain"], 1)
                dve.wait_ge(g["chain"], done[0])

            nc.vector.reduce_sum(tot[:, :, :], ss[:, :, :].rearrange("p (i n) m -> p i m n", i=IMG), AX.X).then_inc(g["tot"], 1)
            dve.wait_ge(g["loaded"], 64)
            nc.vector.tensor_copy(beta[:, :, :], view(gbv[:, 1, 0:1], [[1, MC], [0, 128]])).then_inc(g["beta"], 1)
            dve.wait_ge(g["sums"], 1)
            then(nc.vector.reduce_sum(mean[:, :], psM.rearrange("p (i m) -> p i m", i=IMG), AX.X))
            then(nc.vector.tensor_scalar(mean[:, :], mean[:, :], 1.0 / HID, 1e-6, ALU.mult, ALU.add))
            then(nc.vector.reciprocal(mean[:, :], mean[:, :]))
            for i in range(IMG):
                then(nc.vector.scalar_tensor_tensor(scale[:, i, :], gx[:, i, :], mean[:, i:i + 1], gbv[:, 0, :], ALU.mult, ALU.mult))
            then(nc.vector.tensor_scalar(scale[:, :, :], scale[:, :, :], 1.0, None, ALU.add))
            for i in range(IMG):
                nc.vector.tensor_tensor(gain2[:, i], w2[:, :, :], view(scale[:, i, 0:1], [[1, MC], [0, C]]), ALU.mult)
            dve.wait_ge(g["const"], 1)
            nc.vector.tensor_tensor(cvec[:, :], psC, b2[:, :], ALU.add)


def project(nc, a, d, X, PS, gain2, cvec, stack):
    s = Scope(nc, "down", stack)
    R = BX
    hid = s.sb("hid", [128, R, MC, 128])
    x2 = s.sb("x2", [128, R, C])
    hloaded, xloaded = s.sems("hloaded", R), s.sems("xloaded", R)
    q = {x: s.sem(x) for x in ("resid", "down", "out")}
    with nc.Block() as block:
        @block.sync
        def _(sp):
            def body(b):
                if b.reached(R):
                    sp.wait_ge(q["down"], b.n - R + 1)
                sp.dma_start(hid[:, b.buf(R)], d["hid"][bass.ds(b.n, 1)].rearrange("o p m t -> (o p) m t")).then_inc(hloaded[b.buf(R)], 16)
                if b.reached(R):
                    sp.wait_ge(q["out"], b.n - R + 1)
                sp.dma_start(x2[:, b.buf(R), :], d["x2"][bass.ds(b.n, 1)].rearrange("o p c -> (o p) c")).then_inc(xloaded[b.buf(R)], 16)
            run_steps(sp, NB, R, R, 0, body)

        @block.gpsimd
        def _(pool):
            def body(b):
                pool.wait_ge(xloaded[b.buf(R)], b.turn(R) * 16 + 16)
                nc.gpsimd.tensor_tensor(x2[:, b.buf(R), :], x2[:, b.buf(R), :], cvec[:, :], ALU.add).then_inc(q["resid"], 1)
            run_steps(pool, NB, R, R, 0, body)

        @block.vector
        def _(dve):
            def body(b):
                dve.wait_ge(q["resid"], b.n + 1)
                dve.wait_ge(q["down"], b.n + 1)
                nc.vector.tensor_tensor(at(X, b.n), PS[:, b.buf(R), 0:C], x2[:, b.buf(R), :], ALU.add).then_inc(q["out"], 1)
            run_steps(dve, NB, R, R, 0, body)

        @block.tensor
        def _(pe):
            for img in range(IMG):
                def body(b):
                    b = Step(b.g, b.j + img * PER, R)
                    pe.wait_ge(hloaded[b.buf(R)], b.turn(R) * 16 + 16)
                    if b.reached(R):
                        pe.wait_ge(q["out"], b.n - R + 1)
                    for m in range(MC):
                        last = nc.tensor.matmul(PS[:, b.buf(R), 0:C], hid[:, b.buf(R), m, :], gain2[:, img, m, :], start=(m == 0), stop=(m == MC - 1))
                    last.then_inc(q["down"], 1)
                run_steps(pe, PER, R, R, 0, body)


def build(nc, a, out):
    d = {"x": a["x"]}
    d["x1"] = nc.dram_tensor("scratch_x1", [IMG, C, HW + 2, HW], F32, kind="Internal").ap()
    d["x2"] = nc.dram_tensor("scratch_x2", [NB, 128, C], F32, kind="Internal").ap()
    d["hid"] = nc.dram_tensor("scratch_hid", [NB, 128, MC, 128], F32, kind="Internal").ap()
    d["taps"] = nc.dram_tensor("scratch_taps", [2, 2, C, GSZ], F32, kind="Internal").ap()
    d["bias"] = nc.dram_tensor("scratch_bias", [C], F32, kind="Internal").ap()
    with ExitStack() as stack:
        stack.enter_context(nc.allow_non_contiguous_dma(reason="vectors of 192 to 768 elements, once"))
        prepare(nc, a, d, stack)
    with ExitStack() as whole:
        whole.enter_context(nc.allow_non_contiguous_dma(reason="vectors of 192 to 768 elements, once"))
        X = whole.enter_context(nc.sbuf_tensor("X", [128, NB, C], F32))
        PS = whole.enter_context(nc.psum_tensor("PS", [128, 8, 512], F32))
        with ExitStack() as stack:
            attention(nc, a, d, X, PS, stack)
        with ExitStack() as stack:
            mlp(nc, a, d, X, PS, stack)
        with ExitStack() as stack:
            sobel(nc, a, d, X, PS, stack)
        sems = Scope(nc, "dw", whole)
        convs = ({x: sems.sem(x) for x in ("bloaded", "ready", "mats_a", "mats_b", "xc_ready", "xs_half", "xs_ready", "conv", "result")},
                 sems.sems("loaded", 4))
        with ExitStack() as stack:
            depthwise(nc, "dw7", 0, *convs, d["taps"][0], a["L2_conv_dw_b"], X, PS, None, stack)
        with ExitStack() as both:
            gain2 = both.enter_context(nc.sbuf_tensor("gain2", [128, IMG, MC, C], F32))
            cvec = both.enter_context(nc.sbuf_tensor("cvec", [128, C], F32))
            with nc.sbuf_tensor("ss", [128, NP, MC], F32) as ss:
                with ExitStack() as stack:
                    hidden(nc, a, d, X, PS, ss, stack)
                with ExitStack() as stack:
                    response_norm(nc, a, PS, ss, gain2, cvec, stack)
            with ExitStack() as stack:
                project(nc, a, d, X, PS, gain2, cvec, stack)
        with ExitStack() as stack:
            depthwise(nc, "dw13", 1, *convs, d["taps"][1], d["bias"], X, PS, out, stack)


def kernel(**inputs):
    import numpy as np
    import concourse.bacc as bacc
    from concourse.bass_utils import run_bass_kernel_spmd

    nc = bacc.Bacc("TRN2", target_bir_lowering=False, num_devices=1)
    arrays, a = {}, {}
    for name, v in inputs.items():
        v = np.asarray(v)
        if name == "x":
            v = v.reshape(IMG, C, BY, 8, BX, 2, 8).transpose(0, 2, 4, 5, 3, 6, 1).reshape(NB, 128, C)
        if name == "L1_conv_fusion_w":
            name, v = "L1_conv_fusion_wT", v.T
        if "conv_bn_" in name:
            v = v.T
        v = np.ascontiguousarray(v)
        arrays["in_" + name] = v
        a[name] = nc.dram_tensor("in_" + name, v.shape, mybir.dt.from_np(v.dtype), kind="ExternalInput").ap()
    out = nc.dram_tensor("out", [C, 128, NB], F32, kind="ExternalOutput").ap()
    build(nc, a, out)
    r = run_bass_kernel_spmd(nc, [arrays], core_ids=[0])
    y = r.results[0]["out"].reshape(C, 8, 16, IMG, BY, BX)
    return np.ascontiguousarray(y.transpose(3, 0, 4, 1, 5, 2)).reshape(IMG, C, HW, HW)
```
